# Optimizing a Trainium2 kernel written in Bass

```python
import numpy as np
import jax
import jax.numpy as jnp

def _softmax(x, axis=-1):
    return jax.nn.softmax(x, axis=axis)

def _gelu(x):
    return jax.nn.gelu(x, approximate=True)

def _silu(x):
    return jax.nn.silu(x)

def _sigmoid(x):
    return jax.nn.sigmoid(x)

def _layernorm(x, axis=-1, eps=1e-05):
    m = jnp.mean(x, axis=axis, keepdims=True)
    v = jnp.var(x, axis=axis, keepdims=True)
    return (x - m) / jnp.sqrt(v + eps)

def _scatter_add(tgt, idx, src, axis=0):
    return tgt.at[idx].add(src)

def _segment_sum(src, seg, n):
    return jax.ops.segment_sum(src, seg, n)
kernel_name = 'mk_hybrid_d1_jaxref_r8_488964'

def setup_inputs(seed: int=0):
    np.random.seed(seed)
    _w = jnp.asarray

    def _L0_attn_a_setup():
        import jax, jax.numpy as jnp
        import numpy as np
        EPS = 1e-05
        NUM_HEADS = 16

        def _linear_attention(x, Wq, Wk, Wv, Wo, bo):
            B, L, E = x.shape
            H = NUM_HEADS
            D = E // H
            q = (x @ Wq.T).reshape(B, L, H, D)
            k = (x @ Wk.T).reshape(B, L, H, D)
            v = (x @ Wv.T).reshape(B, L, H, D)
            phi_q = jax.nn.elu(q) + 1.0
            phi_k = jax.nn.elu(k) + 1.0
            pq = jnp.moveaxis(phi_q, 1, 0)
            pk = jnp.moveaxis(phi_k, 1, 0)
            vt = jnp.moveaxis(v, 1, 0)
            S0 = jnp.zeros((B, H, D, D), x.dtype)
            z0 = jnp.zeros((B, H, D), x.dtype)

            def step(carry, inp):
                S, z = carry
                pq_t, pk_t, v_t = inp
                S = S + pk_t[..., :, None] * v_t[..., None, :]
                z = z + pk_t
                num = jnp.einsum('bhd,bhde->bhe', pq_t, S)
                den = jnp.sum(pq_t * z, axis=-1, keepdims=True) + EPS
                return ((S, z), num / den)
            (_, _), out = jax.lax.scan(step, (S0, z0), (pq, pk, vt))
            out = jnp.moveaxis(out, 0, 1).reshape(B, L, E)
            return out @ Wo.T + bo
        key = jax.random.key(seed)
        ks = jax.random.split(key, 6)
        B, L, E = (4, 512, 128)
        s = 1.0 / np.sqrt(E)
        return {'x': jax.random.normal(ks[0], (B, L, E), jnp.float32), 'Wq': jax.random.normal(ks[1], (E, E), jnp.float32) * s, 'Wk': jax.random.normal(ks[2], (E, E), jnp.float32) * s, 'Wv': jax.random.normal(ks[3], (E, E), jnp.float32) * s, 'Wo': jax.random.normal(ks[4], (E, E), jnp.float32) * s, 'bo': jnp.zeros((E,), jnp.float32)}
    _L0_attn_a_in = _L0_attn_a_setup()

    def _L0_attn_b_setup():
        import jax, jax.numpy as jnp
        import numpy as np
        B, N, D_MODEL, H = (4, 256, 128, 16)
        key = jax.random.key(seed)
        k1, k2, k3 = jax.random.split(key, 3)
        x = jax.random.normal(k1, (B, N, D_MODEL), dtype=jnp.float32)
        Wqkv = jax.random.normal(k2, (3 * D_MODEL, D_MODEL), dtype=jnp.float32) * 0.02
        bqkv = jnp.zeros((3 * D_MODEL,), dtype=jnp.float32)
        Wo = jax.random.normal(k3, (D_MODEL, D_MODEL), dtype=jnp.float32) * 0.02
        bo = jnp.zeros((D_MODEL,), dtype=jnp.float32)
        return {'x': x, 'Wqkv': Wqkv, 'bqkv': bqkv, 'Wo': Wo, 'bo': bo}
    _L0_attn_b_in = _L0_attn_b_setup()

    def _L0_ffn_setup():
        import jax, jax.numpy as jnp
        import numpy as np
        B, S, D = (1, 256, 128)
        E, F = (16, 128)
        NG, TKG, K = (4, 2, 4)
        NSH = 2
        SCALE = 2.5
        STD = 0.02
        EPG = E // NG

        def _route(x_flat, router_w, bias):
            logits = x_flat.astype(jnp.float32) @ router_w.T
            scores = jax.nn.sigmoid(logits)
            s = scores + bias[None, :]
            sg = s.reshape(-1, NG, EPG)
            group_score = jax.lax.top_k(sg, 2)[0].sum(-1)
            gidx = jax.lax.top_k(group_score, TKG)[1]
            gmask = jnp.sum(jax.nn.one_hot(gidx, NG, dtype=jnp.float32), axis=1) > 0
            emask = jnp.repeat(gmask, EPG, axis=1)
            masked = jnp.where(emask, s, -1.0)
            topk_idx = jax.lax.top_k(masked, K)[1]
            tw = jnp.take_along_axis(scores, topk_idx, axis=1)
            tw = tw / (tw.sum(-1, keepdims=True) + 1e-20)
            tw = tw * SCALE
            return (topk_idx, tw)
        key = jax.random.key(seed)
        ks = jax.random.split(key, 8)
        return {'hidden_states': jax.random.normal(ks[0], (B, S, D), jnp.float32), 'router_w': jax.random.normal(ks[1], (E, D), jnp.float32) * STD, 'bias': jnp.zeros((E,), jnp.float32), 'gate_w': jax.random.normal(ks[2], (E, D, F), jnp.float32) * STD, 'up_w': jax.random.normal(ks[3], (E, D, F), jnp.float32) * STD, 'down_w': jax.random.normal(ks[4], (E, F, D), jnp.float32) * STD, 'sh_gate_w': jax.random.normal(ks[5], (D, NSH * F), jnp.float32) * STD, 'sh_up_w': jax.random.normal(ks[6], (D, NSH * F), jnp.float32) * STD, 'sh_down_w': jax.random.normal(ks[7], (NSH * F, D), jnp.float32) * STD}
    _L0_ffn_in = _L0_ffn_setup()
    _d = {'L0_attn_a_x': _L0_attn_a_in['x'], 'L0_attn_a_Wq': _L0_attn_a_in['Wq'], 'L0_attn_a_Wk': _L0_attn_a_in['Wk'], 'L0_attn_a_Wv': _L0_attn_a_in['Wv'], 'L0_attn_a_Wo': _L0_attn_a_in['Wo'], 'L0_attn_a_bo': _L0_attn_a_in['bo'], 'L0_attn_b_Wqkv': _L0_attn_b_in['Wqkv'], 'L0_attn_b_bqkv': _L0_attn_b_in['bqkv'], 'L0_attn_b_Wo': _L0_attn_b_in['Wo'], 'L0_attn_b_bo': _L0_attn_b_in['bo'], 'L0_ffn_router_w': _L0_ffn_in['router_w'], 'L0_ffn_bias': _L0_ffn_in['bias'], 'L0_ffn_gate_w': _L0_ffn_in['gate_w'], 'L0_ffn_up_w': _L0_ffn_in['up_w'], 'L0_ffn_down_w': _L0_ffn_in['down_w'], 'L0_ffn_sh_gate_w': _L0_ffn_in['sh_gate_w'], 'L0_ffn_sh_up_w': _L0_ffn_in['sh_up_w'], 'L0_ffn_sh_down_w': _L0_ffn_in['sh_down_w']}
    _x0 = _d['L0_attn_a_x']
    _d['L0_attn_a_x'] = jax.random.normal(jax.random.fold_in(jax.random.key(seed), 1), (8, 256, 128), dtype=_x0.dtype)
    del _x0
    return _d

def reference(L0_attn_a_x, L0_attn_a_Wq, L0_attn_a_Wk, L0_attn_a_Wv, L0_attn_a_Wo, L0_attn_a_bo, L0_attn_b_Wqkv, L0_attn_b_bqkv, L0_attn_b_Wo, L0_attn_b_bo, L0_ffn_router_w, L0_ffn_bias, L0_ffn_gate_w, L0_ffn_up_w, L0_ffn_down_w, L0_ffn_sh_gate_w, L0_ffn_sh_up_w, L0_ffn_sh_down_w):

    def _L0_attn_a_ref(x, Wq, Wk, Wv, Wo, bo):
        import jax, jax.numpy as jnp
        import numpy as np
        EPS = 1e-05
        NUM_HEADS = 16

        def _linear_attention(x, Wq, Wk, Wv, Wo, bo):
            B, L, E = x.shape
            H = NUM_HEADS
            D = E // H
            q = (x @ Wq.T).reshape(B, L, H, D)
            k = (x @ Wk.T).reshape(B, L, H, D)
            v = (x @ Wv.T).reshape(B, L, H, D)
            phi_q = jax.nn.elu(q) + 1.0
            phi_k = jax.nn.elu(k) + 1.0
            pq = jnp.moveaxis(phi_q, 1, 0)
            pk = jnp.moveaxis(phi_k, 1, 0)
            vt = jnp.moveaxis(v, 1, 0)
            S0 = jnp.zeros((B, H, D, D), x.dtype)
            z0 = jnp.zeros((B, H, D), x.dtype)

            def step(carry, inp):
                S, z = carry
                pq_t, pk_t, v_t = inp
                S = S + pk_t[..., :, None] * v_t[..., None, :]
                z = z + pk_t
                num = jnp.einsum('bhd,bhde->bhe', pq_t, S)
                den = jnp.sum(pq_t * z, axis=-1, keepdims=True) + EPS
                return ((S, z), num / den)
            (_, _), out = jax.lax.scan(step, (S0, z0), (pq, pk, vt))
            out = jnp.moveaxis(out, 0, 1).reshape(B, L, E)
            return out @ Wo.T + bo
        return _linear_attention(x, Wq, Wk, Wv, Wo, bo)

    def _L0_attn_b_ref(x, Wqkv, bqkv, Wo, bo):
        import jax, jax.numpy as jnp
        import numpy as np
        B, N, D_MODEL, H = (4, 256, 128, 16)
        b, n, _ = x.shape
        qkv = x @ Wqkv.T + bqkv
        qkv = qkv.reshape(b, n, H, -1).transpose(0, 2, 1, 3)
        q, k, v = jnp.split(qkv, 3, axis=-1)
        scale = k.shape[-1] ** 0.5
        scores = jnp.einsum('bhqd,bhkd->bhqk', q, k) / scale
        attn = jax.nn.softmax(scores, axis=-1)
        out = jnp.einsum('bhqk,bhkd->bhqd', attn, v)
        out = out.transpose(0, 2, 1, 3).reshape(b, n, -1)
        return out @ Wo.T + bo

    def _L0_ffn_ref(hidden_states, router_w, bias, gate_w, up_w, down_w, sh_gate_w, sh_up_w, sh_down_w):
        import jax, jax.numpy as jnp
        import numpy as np
        B, S, D = (1, 256, 128)
        E, F = (16, 128)
        NG, TKG, K = (4, 2, 4)
        NSH = 2
        SCALE = 2.5
        STD = 0.02
        EPG = E // NG

        def _route(x_flat, router_w, bias):
            logits = x_flat.astype(jnp.float32) @ router_w.T
            scores = jax.nn.sigmoid(logits)
            s = scores + bias[None, :]
            sg = s.reshape(-1, NG, EPG)
            group_score = jax.lax.top_k(sg, 2)[0].sum(-1)
            gidx = jax.lax.top_k(group_score, TKG)[1]
            gmask = jnp.sum(jax.nn.one_hot(gidx, NG, dtype=jnp.float32), axis=1) > 0
            emask = jnp.repeat(gmask, EPG, axis=1)
            masked = jnp.where(emask, s, -1.0)
            topk_idx = jax.lax.top_k(masked, K)[1]
            tw = jnp.take_along_axis(scores, topk_idx, axis=1)
            tw = tw / (tw.sum(-1, keepdims=True) + 1e-20)
            tw = tw * SCALE
            return (topk_idx, tw)
        x = hidden_states.reshape(-1, D)
        topk_idx, tw = _route(x, router_w, bias)
        combine = (jax.nn.one_hot(topk_idx, E, dtype=tw.dtype) * tw[..., None]).sum(1)
        h = jnp.einsum('td,edf->etf', x, gate_w)
        u = jnp.einsum('td,edf->etf', x, up_w)
        y = jnp.einsum('etf,efd->etd', jax.nn.silu(h) * u, down_w)
        routed = jnp.einsum('etd,te->td', y, combine)
        sh = jax.nn.silu(x @ sh_gate_w) * (x @ sh_up_w) @ sh_down_w
        return (routed + sh).reshape(hidden_states.shape)
    x = L0_attn_a_x
    x = x + _L0_attn_a_ref(_layernorm(x, axis=-1), L0_attn_a_Wq, L0_attn_a_Wk, L0_attn_a_Wv, L0_attn_a_Wo, L0_attn_a_bo)
    x = x + _L0_ffn_ref(_layernorm(x, axis=-1), L0_ffn_router_w, L0_ffn_bias, L0_ffn_gate_w, L0_ffn_up_w, L0_ffn_down_w, L0_ffn_sh_gate_w, L0_ffn_sh_up_w, L0_ffn_sh_down_w)
    x = x + _L0_attn_b_ref(_layernorm(x, axis=-1), L0_attn_b_Wqkv, L0_attn_b_bqkv, L0_attn_b_Wo, L0_attn_b_bo)
    x = x + _L0_ffn_ref(_layernorm(x, axis=-1), L0_ffn_router_w, L0_ffn_bias, L0_ffn_gate_w, L0_ffn_up_w, L0_ffn_down_w, L0_ffn_sh_gate_w, L0_ffn_sh_up_w, L0_ffn_sh_down_w)
    return x

_drawn_inputs = setup_inputs


def setup_inputs(seed=0):
    import zlib

    import numpy as np

    out = dict(_drawn_inputs(seed))
    spreads = {'L0_attn_a_bo': (0.0, 0.1),
     'L0_attn_b_bqkv': (0.0, 0.434),
     'L0_attn_b_bo': (0.0, 0.1),
     'L0_ffn_bias': (0.0, 0.558)}
    factors = {'L0_attn_b_Wqkv': 7.571,
     'L0_ffn_router_w': 6.006,
     'L0_ffn_gate_w': 4.028,
     'L0_ffn_up_w': 3.983,
     'L0_ffn_down_w': 4.014,
     'L0_ffn_sh_gate_w': 3.547,
     'L0_ffn_sh_up_w': 3.482,
     'L0_ffn_sh_down_w': 3.498}
    for name, (base, spread) in spreads.items():
        noise = np.random.default_rng([zlib.crc32(name.encode()), seed]).standard_normal(out[name].shape)
        drawn = base * np.exp(spread * noise) if base else spread * noise
        out[name] = jnp.asarray(drawn.astype(out[name].dtype))
    for name, factor in factors.items():
        out[name] = (out[name] * factor).astype(out[name].dtype)
    return out
```

```python
import concourse.bass as bass
from concourse import mybir
from contextlib import ExitStack


class NormSems:

    def __init__(self, sem, prefix):
        self.st = sem(prefix + "st")
        self.mv = sem(prefix + "mv")
        self.ve = sem(prefix + "ve")
        self.rs = sem(prefix + "rs")
        self.xn = sem(prefix + "xn")
        self.xt = sem(prefix + "xt")
        self.xs = sem(prefix + "xs")
        self.xl = sem(prefix + "xl")


class AttentionSems:

    def __init__(self, sem, prefix):
        self.xv = sem(prefix + "xv")
        self.vm = sem(prefix + "vm")
        self.vd = sem(prefix + "vd")
        self.bo = sem(prefix + "bo")
        self.pj = sem(prefix + "pj")
        self.rl = sem(prefix + "rl")
        self.ph = sem(prefix + "ph")
        self.hp = sem(prefix + "hp")
        self.qs = sem(prefix + "qs")
        self.s1 = sem(prefix + "s1")
        self.mk = sem(prefix + "mk")
        self.mt = sem(prefix + "mt")
        self.q2 = sem(prefix + "q2")
        self.mx = sem(prefix + "mx")
        self.s2 = sem(prefix + "s2")
        self.ex = sem(prefix + "ex")
        self.pv = sem(prefix + "pv")
        self.ot = sem(prefix + "ot")
        self.nt = sem(prefix + "nt")
        self.dn = sem(prefix + "dn")
        self.rd = sem(prefix + "rd")
        self.nm = sem(prefix + "nm")
        self.e1 = sem(prefix + "e1")
        self.ott = sem(prefix + "ott")
        self.e2 = sem(prefix + "e2")
        self.res = sem(prefix + "res")
        self.e4 = sem(prefix + "e4")
        self.th = sem(prefix + "th")
        self.e5 = sem(prefix + "e5")
        self.rv = sem(prefix + "rv")
        self.cth = sem(prefix + "cth")
        self.ct = sem(prefix + "ct")
        self.cb = sem(prefix + "cb")


class ExpertSems:

    def __init__(self, sem, prefix):
        self.g = sem(prefix + "g")
        self.u = sem(prefix + "u")
        self.c = sem(prefix + "c")
        self.th = sem(prefix + "th")
        self.a = sem(prefix + "a")
        self.b = sem(prefix + "b")
        self.gg = sem(prefix + "gg")
        self.gh = sem(prefix + "gh")
        self.gl = sem(prefix + "gl")
        self.d = sem(prefix + "d")
        self.yt = sem(prefix + "yt")
        self.e1 = sem(prefix + "e1")
        self.res = sem(prefix + "res")


def hybrid_block(nc, ins, out):
    f32 = mybir.dt.float32
    f32r = mybir.dt.float32r
    ALU = mybir.AluOpType
    ACT = mybir.ActivationFunctionType
    AX = mybir.AxisListType

    (x_in, wq_a, wk_a, wv_a, wo_a, bo_a, wqkv_b, bqkv_b, wo_b, bo_b,
     router_w, router_bias, gate_w, up_w, down_w, sh_gate, sh_up, sh_down) = ins

    P = 128
    BATCH, SEQ, DM = x_in.shape
    TOKENS = BATCH * SEQ
    TILES = TOKENS // P
    CT = 4
    CHUNK = CT * P
    CHUNKS = TILES // CT
    H = 16
    HD = DM // H
    HG = 4
    BPC = CHUNK // SEQ
    SLOTS = HG * BPC
    EXPERTS = router_w.shape[0]
    UNITS = EXPERTS + 2
    GROUPS, TOP_GROUPS, TOP_K = 4, 2, 4
    EPG = EXPERTS // GROUPS
    ROUTE_SCALE = 2.5
    LN_EPS = 1e-5
    DEN_EPS = 1e-5
    SOFTMAX_SCALE = float(HD) ** -0.5
    BIG = 3e38
    PIECES, UPP = 6, 3

    x_tiles = x_in.rearrange("b (t p) d -> p (b t) d", p=P)
    out_tiles = out.rearrange("b (t p) d -> p (b t) d", p=P)

    ctx = ExitStack()
    with ctx:
        def sb(name, shape, dt=f32):
            return ctx.enter_context(nc.sbuf_tensor(name, shape, dt))

        def sem(name):
            return ctx.enter_context(nc.semaphore(name))

        X = sb("X", [P, TILES, DM])
        XH = sb("XH", [P, TOKENS], f32r)
        XL = sb("XL", [P, TOKENS], f32r)
        CB = sb("CB", [2 * EXPERTS, TOKENS], f32r)
        WH = sb("WH", [P, UNITS, 3, P], f32r)
        WL = sb("WL", [P, UNITS, 3, P], f32r)
        stage = sb("stage", [P, 2, UPP, 3, P])
        SEL = sb("SEL", [2 * EXPERTS, EXPERTS, P], f32r)
        QS = sb("QS", [P, HG, CHUNK], f32r)
        KS = sb("KS", [P, HG, CHUNK], f32r)
        Q2 = sb("Q2", [P, 2, SEQ], f32r)
        PT = sb("PT", [P, 2, 4, CHUNK])
        V = sb("V", [P, CT, H, 32])
        PHI = sb("PHI", [P, 4, CHUNK])
        HP = sb("HP", [P, 2, CHUNK], f32r)
        OTS = sb("OTS", [P, CHUNK])
        OTOK = sb("OTOK", [P, CT, DM])
        OTT = sb("OTT", [P, CHUNK])
        XN = sb("XN", [P, CT, DM])
        XS = sb("XS", [P, CHUNK])
        XV = sb("XV", [P, CHUNK])
        MEXP = sb("MEXP", [P, 2, P])
        MASK = sb("MASK", [P, 3, P])
        nat = stage[:, 0, :, :, :].rearrange("p a b c -> p (a b) c")
        QKR = PT[:, 0, :, :].rearrange("p a (h c) -> p a h c", c=32)
        SELR = PT[0:2 * EXPERTS, 1, :, :].rearrange("p a (e c) -> p (a e) c", c=P)
        QKH = sb("QKH", [P, 4, H * 32], f32r)
        QKL = sb("QKL", [P, 4, H * 32], f32r)
        WV = sb("WV", [P, 2, DM])
        WO = sb("WO", [P, 2, DM])
        RT = sb("RT", [P, EXPERTS])
        BO = sb("BO", [P, 2, DM])
        BV = sb("BV", [P, H, HD])
        RB = sb("RB", [P, EXPERTS])
        BROW = sb("BROW", [1, 3 * DM])
        SROW = sb("SROW", [1, 2, H * 32])
        MROW = sb("MROW", [1, 2, P])
        COL = sb("COL", [P, 10])
        BCM = sb("BCM", [P, 8])
        ident = sb("ident", [P, P])
        STT_ = sb("LNST", [P, CT, 6])
        MV = sb("MV", [P, CT, 2])
        VE = sb("VE", [P, CT])
        RS = sb("RS", [P, CT])
        NH = sb("NH", [P, CT])
        EPS = sb("EPS", [P, CT])
        junk = sb("junk", [P, 1])
        DEN = sb("DEN", [P, CT, 4])
        RDEN = sb("RDEN", [P, CT, 4])
        TH64 = sb("TH64", [P, CT, EXPERTS])
        SC = sb("SC", [P, CT, EXPERTS])
        SBI = sb("SBI", [P, CT, EXPERTS])
        PMX = sb("PMX", [P, CT * GROUPS, 2])
        PMN = sb("PMN", [P, CT * GROUPS, 2])
        T1 = sb("T1", [P, CT * GROUPS])
        T2 = sb("T2", [P, CT * GROUPS])
        T3 = sb("T3", [P, CT * GROUPS])
        GE = sb("GE", [P, CT, GROUPS + 8 - TOP_GROUPS])
        GM = sb("GM", [P, CT, 8])
        GR = sb("GR", [P, CT, GROUPS + 8 - TOP_GROUPS])
        GMK = sb("GMK", [P, CT, GROUPS])
        T4 = sb("T4", [P, CT, EXPERTS])
        ME = sb("ME", [P, CT, EXPERTS + 8 - TOP_K])
        EM = sb("EM", [P, CT, 8])
        ER = sb("ER", [P, CT, EXPERTS + 8 - TOP_K])
        W = sb("W", [P, CT, EXPERTS])
        SM = sb("SM", [P, CT])
        SME = sb("SME", [P, CT])
        RSM = sb("RSM", [P, CT])
        C = sb("C", [P, CT, EXPERTS])
        CTK = sb("CTK", [P, CT, 2 * EXPERTS])
        TH = PT[:, 0, 0:2, :]
        AB = PT[:, 0, 2:4, :]
        GG = PT[:, 1, 0:3, :]
        GH = QS[:, 0:3, :]
        GL = KS[:, 0:3, :]

        BANK = [ctx.enter_context(nc.psum_tensor(f"bank{i}", [P, 512], f32)) for i in range(8)]
        S = BANK[0:4]
        OT, PJ, MT, TP = BANK[4:8]
        G = BANK[0:2]
        U = BANK[2:4]
        CBC = BANK[4:6]
        Y = BANK[6]

        s_x = sem("x_loaded")
        s_nat = sem("small_weights_loaded")
        s_row = sem("bias_row_loaded")
        s_bc = sem("broadcasts_loaded")
        s_raw = [sem(f"piece{p}_loaded") for p in range(PIECES)]
        s_wh = sem("piece_high_done")
        s_wl = sem("piece_low_done")
        s_id = sem("ident_done")
        s_pc = sem("pool_constants_done")
        s_wt = sem("weights_transposed")
        s_w0 = sem("bank0_unpacked")
        s_w1 = sem("bank1_unpacked")
        s_row2s = sem("rows_cleared")
        s_row2 = sem("rows_done")
        s_sel = sem("selectors_done")
        s_col = sem("columns_transposed")
        s_cd = sem("columns_done")
        s_qkh = sem("qk_high_done")
        s_qkl = sem("qk_low_done")
        s_out = sem("stored")

        LN = [NormSems(sem, f"ln{k}_") for k in range(4)]
        AT = [AttentionSems(sem, f"at{k}_") for k in range(2)]
        FF = [ExpertSems(sem, f"ff{k}_") for k in range(2)]

        def ch(t, c, n):
            return t[:, bass.ds(c * n, n)]

        def tiles(c):
            return X[:, bass.ds(c * CT, CT), :]

        def flat(ap):
            return ap.rearrange("p a b c -> p (a b c)")

        def group_of(g, lag):
            return ((g - lag) % SLOTS) // BPC, (g - lag) % BPC

        def chunks(eng, body):
            body(0, True, False)
            with eng.Fori(1, CHUNKS) as c:
                body(c, True, True)
            body(CHUNKS, False, True)

        block = ctx.enter_context(nc.Block())

        @block.sync
        def _(sp):
            for m, w in enumerate((wq_a, wk_a, wv_a, wo_a)):
                sp.dma_start(nat[:, m, :], w).then_inc(s_nat, 16)
            sp.dma_start(X[:, :, :], x_tiles).then_inc(s_x, 16)

            def piece(p):
                dst = stage[:, p % 2, :, :, :]
                if p == 0:
                    sp.wait_ge(s_wt, 1)
                if p >= 2:
                    sp.wait_ge(s_wl, p - 1)
                e0 = p * UPP
                n = min(UPP, EXPERTS - e0)
                for k, w in enumerate((gate_w, up_w, down_w)):
                    sp.dma_start(dst[:, 0:n, k, :], w[e0:e0 + n].rearrange("e d f -> d e f")).then_inc(s_raw[p], 16)
                if n < UPP:
                    for k, w in enumerate((sh_gate, sh_up)):
                        sp.dma_start(dst[:, n:UPP, k, :], w.rearrange("d (a f) -> d a f", a=2)).then_inc(s_raw[p], 16)
                    sp.dma_start(dst[:, n:UPP, 2, :], sh_down.rearrange("(a f) d -> f a d", a=2)).then_inc(s_raw[p], 16)

            for p in range(PIECES):
                piece(p)
            with sp.Fori(0, CHUNKS) as c:
                sp.wait_ge(FF[1].res, c + 1)
                sp.dma_start(out_tiles[:, bass.ds(c * CT, CT), :], X[:, bass.ds(c * CT, CT), :]).then_inc(s_out, 16)
            sp.wait_ge(s_out, 16 * CHUNKS)

        @block.gpsimd
        def _(pool):
            pool.memset(ident[:, :], 0.0).then_inc(s_id, 1)
            pool.wait_ge(s_id, 1)
            pool.affine_select(out=ident[:, :], in_=ident[:, :], compare_op=ALU.not_equal, fill=1.0, base=0,
                               pattern=[[-1, P]], channel_multiplier=1).then_inc(s_id, 1)
            pool.memset(QKR, 0.0).then_inc(s_pc, 1)
            pool.memset(V[:, :, :, :], 0.0)
            pool.memset(NH[:, :], -0.5)
            pool.memset(EPS[:, :], LN_EPS)
            pool.memset(MEXP[:, :, :], 0.0)
            pool.memset(GE[:, :, :], BIG)
            pool.memset(ME[:, :, :], BIG)
            pool.memset(SELR, 0.0)
            pool.memset(MASK[:, :, :], 1.0).then_inc(s_pc, 1)
            pool.wait_ge(s_pc, 2)
            pool.memset(V[:, :, :, HD:HD + 1], 1.0)
            for k in (0, 2):
                pool.affine_select(out=MASK[:, k, :], in_=MASK[:, k, :], compare_op=ALU.is_ge, fill=0.0, base=0,
                                   pattern=[[1, P]], channel_multiplier=-1)
            for k in range(2):
                pool.affine_select(out=SELR, in_=SELR, compare_op=ALU.not_equal, fill=1.0, base=-EXPERTS * k,
                                   pattern=[[-1, EXPERTS], [0, P]], channel_multiplier=1).then_inc(s_pc, 1)
                pool.wait_ge(s_pc, 3 + k)

            def norm_pool(L, c):
                pool.wait_ge(L.mv, c + 1)
                pool.tensor_tensor(VE[:, :], MV[:, :, 1], EPS[:, :], ALU.add).then_inc(L.ve, 1)
                pool.wait_ge(L.ve, c + 1)
                pool.tensor_tensor(RS[:, :], VE[:, :], NH[:, :], ALU.pow).then_inc(L.rs, 1)

            with pool.Fori(0, CHUNKS) as c:
                norm_pool(LN[0], c)

            def attention(k, A, L, Lnext):
                def body(c, cur, prev):
                    for g in range(SLOTS):
                        n = c * SLOTS + g
                        if k == 0 and not prev and g >= SLOTS - PIECES:
                            p = g - (SLOTS - PIECES)
                            part = slice(UPP * p, UPP * (p + 1))
                            pool.wait_ge(s_wh, p + 1)
                            pool.tensor_tensor(flat(WL[:, part, :, :]), flat(stage[:, p % 2, :, :, :]),
                                               flat(WH[:, part, :, :]).bitcast(f32), ALU.subtract).then_inc(s_wl, 1)
                        if cur and k == 0:
                            hg, b = group_of(g, 0)
                            pool.wait_ge(A.hp, n + 1)
                            if prev:
                                pool.wait_ge(A.s1, 4 * (n - b - 6))
                            pool.tensor_tensor((KS if b else QS)[:, hg, :], PHI[:, 2 + g % 2, :],
                                               HP[:, g % 2, :].bitcast(f32), ALU.subtract).then_inc(A.qs, 1)
                        if cur and g == 2:
                            pool.wait_ge(L.xl, c + 1)
                            if prev:
                                pool.wait_ge(A.vm, c)
                            pool.tensor_tensor(XV[:, :], ch(XH, c, CHUNK).bitcast(f32), ch(XL, c, CHUNK).bitcast(f32),
                                               ALU.add).then_inc(A.xv, 1)
                            if not prev:
                                pool.wait_ge(s_bc, 16 * 4)
                            pool.tensor_tensor(tiles(c), tiles(c), BO[:, k, :].unsqueeze(1).broadcast_to([P, CT, DM]),
                                               ALU.add).then_inc(A.bo, 1)
                        if prev and g == 5:
                            norm_pool(Lnext, c - 1)

                chunks(pool, body)

            def experts(k, F, Lnext):
                def body(c, cur, prev):
                    for u in range(UNITS):
                        n = c * UNITS + u
                        if cur if u >= 1 else prev:
                            pool.wait_ge(F.gh, n)
                            if u >= 4 or prev:
                                pool.wait_ge(F.d, n - 3)
                            pool.tensor_tensor(GL[:, (u - 1) % 3, :], GG[:, (u - 1) % 3, :],
                                               GH[:, (u - 1) % 3, :].bitcast(f32), ALU.subtract).then_inc(F.gl, 1)
                        if prev and u == 7 and k == 0:
                            norm_pool(Lnext, c - 1)

                chunks(pool, body)

            attention(0, AT[0], LN[0], LN[1])
            experts(0, FF[0], LN[2])
            attention(1, AT[1], LN[2], LN[3])
            experts(1, FF[1], None)

        @block.scalar
        def _(act):
            for m in range(3):
                act.dma_start(nat[:, 4 + m, :], wqkv_b[m * P:(m + 1) * P, :]).then_inc(s_nat, 16)
            act.dma_start(nat[:, 7, :], wo_b).then_inc(s_nat, 16)
            act.dma_start(nat[0:EXPERTS, 8, :], router_w).then_inc(s_nat, 16)
            act.dma_start(BROW[:, :], bqkv_b.rearrange("(a n) -> a n", a=1)).then_inc(s_row, 16)
            act.dma_start(BO[:, 0, :], bo_a.partition_broadcast(P)).then_inc(s_bc, 16)
            act.dma_start(BO[:, 1, :], bo_b.partition_broadcast(P)).then_inc(s_bc, 16)
            act.dma_start(RB[:, :], router_bias.partition_broadcast(P)).then_inc(s_bc, 16)
            act.dma_start(BV[:, :, :], bqkv_b.rearrange("(h c) -> h c", h=H)[:, 2 * HD:3 * HD].partition_broadcast(P))\
               .then_inc(s_bc, 16)
            act.wait_ge(s_wt, 1)
            act.wait_ge(s_pc, 1)
            wqkv_t = BANK[1][:, 0:3 * DM].rearrange("p (h c) -> p h c", h=H)
            for s in range(3):
                act.activation(QKR[:, 2, :, HD * s:HD * (s + 1)], wqkv_t[:, :, 0:HD], ACT.Copy)
                act.activation(QKR[:, 3, :, HD * s:HD * (s + 1)], wqkv_t[:, :, HD:2 * HD], ACT.Copy)
            act.activation(WV[:, 1, :].rearrange("p (h c) -> p h c", h=H), wqkv_t[:, :, 2 * HD:3 * HD], ACT.Copy)
            act.activation(WO[:, 1, :], BANK[1][:, 3 * DM:4 * DM], ACT.Copy).then_inc(s_w1, 1)
            act.wait_ge(s_w0, 1)
            act.wait_ge(s_w1, 1)
            act.activation(QKH[:, :, :], QKR.rearrange("p a h c -> p a (h c)"), ACT.Copy).then_inc(s_qkh, 1)

            def halves(L, c, router):
                act.wait_ge(L.xt, c + 1)
                i = act.activation(ch(XH, c, CHUNK), TP[:, :], ACT.Copy)
                if router:
                    i = act.activation(XS[:, :], TP[:, :], ACT.Copy)
                i.then_inc(L.xs, 1)

            with act.Fori(0, CHUNKS) as c:
                halves(LN[0], c, False)

            def attention(k, A, L, Lnext):
                def body(c, cur, prev):
                    for g in range(SLOTS):
                        n = c * SLOTS + g
                        if k == 0 and not prev and g >= SLOTS - PIECES:
                            p = g - (SLOTS - PIECES)
                            act.wait_ge(s_raw[p], 16 * (6 if p == PIECES - 1 else 3))
                            act.activation(flat(WH[:, UPP * p:UPP * (p + 1), :, :]), flat(stage[:, p % 2, :, :, :]),
                                           ACT.Copy).then_inc(s_wh, 1)
                        hg, b = group_of(g, 0)
                        if cur and k == 0:
                            act.wait_ge(A.pj, n + 1)
                            if g or prev:
                                act.wait_ge(A.ph, n)
                            act.activation(PHI[:, 0, :], PJ[:, :], ACT.Exp)
                            act.activation(PHI[:, 1, :], PJ[:, :], ACT.Relu).then_inc(A.rl, 1)
                        if cur and k == 1:
                            act.wait_ge(A.pj, n + 1)
                            if g >= 2 or prev:
                                act.wait_ge(A.qs, n - 1)
                            if g == 0 and not prev:
                                act.wait_ge(s_cd, 2)
                            act.activation(HP[:, g % 2, :], PJ[:, :], ACT.Identity, bias=BCM[:, 4 * b + hg:4 * b + hg + 1],
                                           scale=COL[:, 8 + b:9 + b]).then_inc(A.hp, 1)
                        if g % 2 == 1 and (cur if g >= 4 else prev):
                            act.wait_ge(A.pv, n - 3)
                            if g >= 7 or prev:
                                act.wait_ge(A.nt, c * HG + (g - 5) // 2)
                            act.activation(OTS[:, :], OT[:, :], ACT.Copy).then_inc(A.ot, 1)
                        if cur and k == 0:
                            if g == 0 and not prev:
                                act.wait_ge(s_cd, 1)
                            act.wait_ge(A.ph, n + 1)
                            if g >= 2 or prev:
                                act.wait_ge(A.qs, n - 1)
                            act.activation(HP[:, g % 2, :], PHI[:, 2 + g % 2, :], ACT.Identity,
                                           scale=COL[:, 8 + b:9 + b]).then_inc(A.hp, 1)
                        if prev and g == 7:
                            act.wait_ge(A.e4, c)
                            act.activation(TH64[:, :, :].rearrange("p a b -> p (a b)"), TP[:, 0:CT * EXPERTS], ACT.Tanh,
                                           scale=0.5).then_inc(A.th, 1)
                        if k == 1 and (cur if g >= 3 else prev):
                            for h in range(4):
                                act.wait_ge(A.s2, 4 * (n - 3) + h + 1)
                                if h == 0 and (g >= 5 or prev):
                                    act.wait_ge(A.pv, n - 4)
                                act.activation(PT[:, (g + 1) % 2, h, :], S[h][:, :], ACT.Exp, scale=SOFTMAX_SCALE)\
                                   .then_inc(A.ex, 1)
                        if prev and g == 4:
                            act.wait_ge(A.e1, c)
                            act.activation(OTT[:, :], TP[:, :], ACT.Copy).then_inc(A.ott, 1)
                        if prev and g == 6:
                            halves(Lnext, c - 1, True)
                        if prev and g == 7:
                            act.wait_ge(A.e5, c)
                            act.activation(ch(CB, c - 1, CHUNK), TP[0:2 * EXPERTS, :], ACT.Copy).then_inc(A.cb, 1)

                chunks(act, body)

            def experts(k, F, Lnext):
                def body(c, cur, prev):
                    for u in range(UNITS):
                        n = c * UNITS + u
                        if cur:
                            act.wait_ge(F.g, n + 1)
                            if u >= 2 or prev:
                                act.wait_ge(F.a, n - 1)
                            act.activation(TH[:, u % 2, :], G[u % 2][:, :], ACT.Tanh, scale=0.5).then_inc(F.th, 1)
                        if cur if u >= 1 else prev:
                            act.wait_ge(F.gg, n)
                            if u >= 4 or prev:
                                act.wait_ge(F.d, n - 3)
                            act.activation(GH[:, (u - 1) % 3, :], GG[:, (u - 1) % 3, :], ACT.Copy).then_inc(F.gh, 1)
                        if prev and u == 2:
                            act.wait_ge(F.d, UNITS * c)
                            act.activation(OTT[:, :], Y[:, :], ACT.Copy).then_inc(F.yt, 1)
                        if prev and u == 10 and k == 0:
                            halves(Lnext, c - 1, False)

                chunks(act, body)

            attention(0, AT[0], LN[0], LN[1])
            experts(0, FF[0], LN[2])
            attention(1, AT[1], LN[2], LN[3])
            experts(1, FF[1], None)

        @block.tensor
        def _(pe):
            def three(out, wh, wl, vh, vl, start=True, stop=True):
                pe.matmul(out, wh, vh, start=start, stop=False)
                pe.matmul(out, wh, vl, start=False, stop=False)
                return pe.matmul(out, wl, vh, start=False, stop=stop)

            pe.wait_ge(s_id, 2)
            pe.wait_ge(s_row2, 1)
            for w in range(2):
                for hg in range(HG):
                    pe.matmul(BANK[2][:, 16 + 4 * w + hg:17 + 4 * w + hg], SROW[:, w, P * hg:P * (hg + 1)], ident[0:1, 0:1],
                              start=True, stop=True)
                i = pe.matmul(BANK[2][:, 24 + w:25 + w], MROW[:, w, :], ident[0:1, 0:1], start=True, stop=True)
            i.then_inc(s_col, 1)
            pe.wait_ge(s_nat, 16 * 9)
            for m in range(8):
                pe.transpose(BANK[m // 4][:, P * (m % 4):P * (m % 4 + 1)], nat[:, m, :], ident[:, :])
            pe.transpose(BANK[3][:, 0:EXPERTS], nat[0:EXPERTS, 8, :], ident[0:EXPERTS, 0:EXPERTS]).then_inc(s_wt, 1)

            def turn(L, c):
                for t in range(CT):
                    i = pe.transpose(TP[:, P * t:P * (t + 1)], XN[:, t, :], ident[:, :])
                i.then_inc(L.xt, 1)

            with pe.Fori(0, CHUNKS) as c:
                pe.wait_ge(LN[0].xn, c + 1)
                turn(LN[0], c)

            def attention(k, A, L, Lnext):
                done, rows = (A.mk, 3 * HD) if k == 0 else (A.ex, 3 * HD + 1)

                def body(c, cur, prev):
                    for g in range(SLOTS):
                        n = c * SLOTS + g
                        if cur:
                            hg, b = group_of(g, 0)
                            if g == 0:
                                pe.wait_ge(L.xl, c + 1)
                            if g or prev:
                                pe.wait_ge(A.rl if k == 0 else A.qs, n)
                            w = slice(P * hg, P * (hg + 1))
                            three(PJ[:, :], QKH[:, 2 * k + b, w], QKL[:, 2 * k + b, w], ch(XH, c, CHUNK), ch(XL, c, CHUNK))\
                                .then_inc(A.pj, 1)
                        if prev and g == 5:
                            pe.wait_ge(A.ott, c)
                            for t in range(CT):
                                i = pe.matmul(TP[:, P * t:P * (t + 1)], OTT[:, P * t:P * (t + 1)], WO[:, k, :],
                                              start=True, stop=True)
                            i.then_inc(A.e2, 1)
                        if k == 1 and (cur if g >= 3 else prev):
                            pe.wait_ge(A.mx, 4 * (n - 2))
                            if g >= 4 or prev:
                                pe.wait_ge(A.q2, n - 3)
                            for t in range(2):
                                i = pe.transpose(MT[:, P * t:P * (t + 1)], MEXP[:, t, :], ident[:, :])
                            i.then_inc(A.mt, 1)

                        def values_product():
                            if not (cur if g >= 4 else prev):
                                return
                            hg, b = group_of(g, 4)
                            pe.wait_ge(done, 4 * (n - 3))
                            if g == 4:
                                pe.wait_ge(A.vd, c + 1)
                            if b == 0 and (g > 4 or prev):
                                pe.wait_ge(A.ot, c * HG + (g - 4) // 2)
                            for kt in range(2):
                                q0 = kt * P if k == 0 else 0
                                for h in range(4):
                                    src = PT[:, g % 2, h, SEQ * kt:SEQ * (kt + 1) - q0]
                                    i = pe.matmul(OT[32 * h:32 * (h + 1), SEQ * b + q0:SEQ * (b + 1)],
                                                  V[:, 2 * b + kt, 4 * hg + h, :], src, start=(kt == 0), stop=(kt == 1),
                                                  skip_group_check=True)
                            i.then_inc(A.pv, 1)

                        if k == 0:
                            values_product()
                        if cur if g >= 2 else prev:
                            hg, b = group_of(g, 2)
                            pe.wait_ge(A.qs, c * SLOTS + (g - 2) // 2 * 2 + 2)
                            for h in range(4):
                                r = slice(32 * h, 32 * h + 3 * HD)
                                if k == 0:
                                    if g >= 3 or prev:
                                        pe.wait_ge(A.mk, 4 * (n - 3) + h + 1)
                                    pe.matmul(S[h][:, 0:SEQ], KS[r, hg, SEQ * b:SEQ * b + P], QS[r, hg, SEQ * b:SEQ * (b + 1)],
                                              start=True, stop=True)
                                    i = pe.matmul(S[h][:, SEQ:SEQ + P], KS[r, hg, SEQ * b + P:SEQ * (b + 1)],
                                                  QS[r, hg, SEQ * b + P:SEQ * (b + 1)], start=True, stop=True)
                                else:
                                    if g >= 4 or prev:
                                        pe.wait_ge(A.ex, 4 * (n - 4) + h + 1)
                                    elif g == 3:
                                        pe.wait_ge(A.mx, 4 * (n - 3) + h + 1)
                                    for t in range(2):
                                        i = pe.matmul(S[h][:, SEQ * t:SEQ * (t + 1)],
                                                      QS[r, hg, SEQ * b + P * t:SEQ * b + P * (t + 1)],
                                                      KS[r, hg, SEQ * b:SEQ * (b + 1)], start=True, stop=True)
                                i.then_inc(A.s1, 1)
                        if g % 2 == 0 and (cur if g >= 6 else prev):
                            j = c * HG + (g - 6) // 2
                            pe.wait_ge(A.ot, j + 1)
                            if g == 0:
                                pe.wait_ge(A.nm, j)
                                if cur:
                                    pe.wait_ge(A.rl if k == 0 else A.hp, n + 1)
                                else:
                                    pe.wait_ge(A.cb, c - 1)
                            if g == 2 or (g == 4 and not cur):
                                pe.wait_ge(A.nm, j)
                            if g == 4 and cur:
                                pe.wait_ge(A.vd, c + 1)
                            if g == 6:
                                pe.wait_ge(A.vd, c + 1)
                                if prev:
                                    pe.wait_ge(A.res, c)
                            for t in range(CT):
                                i = pe.transpose(TP[:, P * t:P * (t + 1)], OTS[:, P * t:P * (t + 1)], ident[:, :])
                            i.then_inc(A.nt, 1)
                        if prev and g == 7:
                            pe.wait_ge(Lnext.xl, c)
                            for t in range(CT):
                                i = pe.matmul(TP[:, EXPERTS * t:EXPERTS * (t + 1)], XS[:, P * t:P * (t + 1)], RT[:, :],
                                              start=True, stop=True)
                            i.then_inc(A.e4, 1)
                        if k == 1:
                            values_product()
                        if k == 1 and (cur if g >= 3 else prev):
                            hg, b = group_of(g, 3)
                            pe.wait_ge(A.q2, n - 2)
                            for h in range(4):
                                r = slice(32 * h, 32 * h + rows)
                                if cur or g < 2:
                                    pe.wait_ge(A.mx, 4 * (n - 2) + h + 1)
                                else:
                                    pe.wait_ge(A.ex, 4 * (n - 4) + h + 1)
                                for t in range(2):
                                    i = pe.matmul(S[h][:, SEQ * t:SEQ * (t + 1)],
                                                  KS[r, hg, SEQ * b + P * t:SEQ * b + P * (t + 1)],
                                                  Q2[r, (g + 1) % 2, :], start=True, stop=True)
                                i.then_inc(A.s2, 1)
                        if cur and g == 3:
                            pe.wait_ge(A.xv, c + 1)
                            if prev:
                                pe.wait_ge(A.nm, c * HG - 1)
                            for t in range(CT):
                                i = pe.matmul(TP[:, P * t:P * (t + 1)], XV[:, P * t:P * (t + 1)], WV[:, k, :],
                                              start=True, stop=True)
                            i.then_inc(A.vm, 1)
                        if prev and g == 4:
                            pe.wait_ge(A.nm, c * HG)
                            for t in range(CT):
                                i = pe.transpose(TP[:, P * t:P * (t + 1)], OTOK[:, t, :], ident[:, :])
                            i.then_inc(A.e1, 1)
                        if prev and g == 6:
                            pe.wait_ge(Lnext.xn, c)
                            if cur:
                                pe.wait_ge(A.nm, c * HG + 1)
                            turn(Lnext, c - 1)
                        if prev and g == 7:
                            pe.wait_ge(A.ct, c)
                            for t in range(CT):
                                i = pe.transpose(TP[0:2 * EXPERTS, P * t:P * (t + 1)], CTK[:, t, :], ident[:, :])
                            i.then_inc(A.e5, 1)

                chunks(pe, body)

            def experts(k, F, A, L, Lnext):
                def body(c, cur, prev):
                    for u in range(UNITS):
                        n = c * UNITS + u
                        if cur:
                            if u == 0:
                                pe.wait_ge(L.xl, c + 1)
                                pe.wait_ge(A.cb, c + 1)
                            vh, vl = ch(XH, c, CHUNK), ch(XL, c, CHUNK)
                            if u >= 2 or prev:
                                pe.wait_ge(F.a, n - 1)
                            three(G[u % 2][:, :], WH[:, u, 0, :], WL[:, u, 0, :], vh, vl).then_inc(F.g, 1)
                            if u >= 2 or prev:
                                pe.wait_ge(F.b, n - 1)
                            if u < EXPERTS:
                                if u >= 2:
                                    pe.wait_ge(F.gg, n - 1)
                                elif prev:
                                    pe.wait_ge(F.gg, n - 3)
                            three(U[u % 2][:, :], WH[:, u, 1, :], WL[:, u, 1, :], vh, vl).then_inc(F.u, 1)
                            if u < EXPERTS:
                                pe.matmul(CBC[u % 2][:, :], SEL[:, u, :], ch(CB, c, CHUNK), start=True, stop=True)\
                                  .then_inc(F.c, 1)
                        if cur if u >= 3 else prev:
                            du = (u - 3) % UNITS
                            pe.wait_ge(F.gl, n - 2)
                            if du == 0 and prev:
                                pe.wait_ge(F.yt, c)
                            three(Y[:, :], WH[:, du, 2, :], WL[:, du, 2, :], GH[:, du % 3, :], GL[:, du % 3, :],
                                  start=(du == 0), stop=(du == UNITS - 1)).then_inc(F.d, 1)
                        if prev and u == 4:
                            pe.wait_ge(F.yt, c)
                            for t in range(CT):
                                i = pe.transpose(TP[:, P * t:P * (t + 1)], OTT[:, P * t:P * (t + 1)], ident[:, :])
                            i.then_inc(F.e1, 1)
                        if prev and u == 9 and k == 0:
                            pe.wait_ge(Lnext.xn, c)
                            turn(Lnext, c - 1)

                chunks(pe, body)

            pe.wait_ge(s_qkl, 1)
            pe.wait_ge(s_cd, 1)
            pe.wait_ge(LN[0].xl, CHUNKS)
            attention(0, AT[0], LN[0], LN[1])
            pe.wait_ge(s_wl, PIECES)
            pe.wait_ge(AT[0].mk, 4 * SLOTS * CHUNKS)
            pe.wait_ge(AT[0].cb, CHUNKS)
            experts(0, FF[0], AT[0], LN[1], LN[2])
            pe.wait_ge(FF[0].gg, UNITS * CHUNKS)
            pe.wait_ge(FF[0].yt, CHUNKS)
            pe.wait_ge(LN[2].xl, CHUNKS)
            attention(1, AT[1], LN[2], LN[3])
            pe.wait_ge(AT[1].ex, 4 * SLOTS * CHUNKS)
            pe.wait_ge(AT[1].cb, CHUNKS)
            experts(1, FF[1], AT[1], LN[3], None)

        @block.vector
        def _(dve):
            dve.memset(SROW[:, :, :], 0.0)
            dve.memset(MROW[:, :, :], 0.0).then_inc(s_row2s, 1)
            dve.wait_ge(s_row2s, 1)
            srow = SROW[:, :, :].rearrange("p w (h c) -> p w h c", h=H)
            mrow = MROW[:, :, :].rearrange("p w (h c) -> p w h c", h=4)
            brow = BROW[:, :].rearrange("p (h c) -> p h c", h=H)
            dve.memset(srow[:, 1, :, 3 * HD:3 * HD + 1], -1.0)
            dve.memset(mrow[:, 0, :, 2 * HD:3 * HD], 1.0)
            dve.memset(mrow[:, 1, :, HD:2 * HD], 1.0)
            dve.wait_ge(s_row, 16)
            for w in range(2):
                for s in range(3):
                    i = dve.tensor_copy(srow[:, w, :, HD * s:HD * (s + 1)], brow[:, :, HD * w:HD * (w + 1)])
            i.then_inc(s_row2, 1)
            dve.wait_ge(s_col, 1)
            dve.tensor_copy(COL[:, :], BANK[2][:, 16:26]).then_inc(s_cd, 1)
            dve.wait_ge(s_cd, 1)
            for w in range(2):
                i = dve.tensor_scalar(BCM[:, 4 * w:4 * (w + 1)], COL[:, 4 * w:4 * (w + 1)], COL[:, 8 + w:9 + w], None, ALU.mult)
            i.then_inc(s_cd, 1)
            dve.wait_ge(s_wt, 1)
            dve.wait_ge(s_pc, 1)
            for w in range(2):
                src = BANK[0][:, DM * w:DM * (w + 1)].rearrange("p (h c) -> p h c", h=H)
                for s in range(3):
                    dve.tensor_copy(QKR[:, w, :, HD * s:HD * (s + 1)], src)
            dve.tensor_copy(WV[:, 0, :], BANK[0][:, 2 * DM:3 * DM])
            dve.tensor_copy(WO[:, 0, :], BANK[0][:, 3 * DM:4 * DM])
            dve.tensor_copy(RT[:, :], BANK[3][:, 0:EXPERTS]).then_inc(s_w0, 1)
            dve.wait_ge(s_pc, 4)
            dve.tensor_copy(SEL[:, :, :], SELR).then_inc(s_sel, 1)

            def norm_stats(L, c):
                dve.memset(junk[:, :], 0.0)
                for t in range(CT):
                    i = dve.bn_stats(out=STT_[:, t, :], in_=X[:, bass.ds(c * CT + t, 1), :].rearrange("p a d -> p (a d)"))
                i.then_inc(L.st, 1)

            def norm_aggregate(L, c):
                dve.wait_ge(L.st, c + 1)
                dve.memset(junk[:, :], 0.0)
                for t in range(CT):
                    i = dve.bn_aggr(out=MV[:, t, :], in_=STT_[:, t, :])
                i.then_inc(L.mv, 1)

            def norm_apply(L, c):
                dve.wait_ge(L.mv, c + 1)
                dve.wait_ge(L.rs, c + 1)
                for t in range(CT):
                    i = dve.tensor_scalar(XN[:, t, :], X[:, bass.ds(c * CT + t, 1), :].rearrange("p a d -> p (a d)"),
                                          MV[:, t, 0:1], RS[:, t:t + 1], ALU.subtract, ALU.mult)
                i.then_inc(L.xn, 1)

            def low_half(L, c):
                dve.wait_ge(L.xs, c + 1)
                dve.tensor_tensor(ch(XL, c, CHUNK), TP[:, :], ch(XH, c, CHUNK).bitcast(f32), ALU.subtract).then_inc(L.xl, 1)

            dve.wait_ge(s_x, 16)
            with dve.Fori(0, CHUNKS) as c:
                norm_stats(LN[0], c)
                norm_aggregate(LN[0], c)
                norm_apply(LN[0], c)
                low_half(LN[0], c)
            dve.wait_ge(s_qkh, 1)
            dve.tensor_tensor(QKL[:, :, :], QKR.rearrange("p a h c -> p a (h c)"), QKH[:, :, :].bitcast(f32),
                              ALU.subtract).then_inc(s_qkl, 1)

            LINKS = 19

            def route(A, c, part):
                base = c * LINKS

                def link(k, instr):
                    instr.then_inc(A.rv, 1)

                def after(k):
                    dve.wait_ge(A.rv, base + k)

                sbi4 = SBI[:, :, :].rearrange("p t (g i j) -> p (t g) i j", i=2, j=2)
                if part == 0:
                    dve.wait_ge(A.th, c + 1)
                    link(1, dve.tensor_scalar(SC[:, :, :], TH64[:, :, :], 0.5, 0.5, ALU.mult, ALU.add))
                    after(1)
                    link(2, dve.tensor_tensor(SBI[:, :, :], SC[:, :, :], RB[:, :].unsqueeze(1).broadcast_to([P, CT, EXPERTS]),
                                              ALU.add))
                if part == 1:
                    after(2)
                    dve.tensor_tensor(PMX[:, :, :], sbi4[:, :, :, 0], sbi4[:, :, :, 1], ALU.max)
                    link(3, dve.tensor_tensor(PMN[:, :, :], sbi4[:, :, :, 0], sbi4[:, :, :, 1], ALU.min))
                    after(3)
                    dve.tensor_tensor(T1[:, :], PMX[:, :, 0], PMX[:, :, 1], ALU.max)
                    dve.tensor_tensor(T2[:, :], PMX[:, :, 0], PMX[:, :, 1], ALU.min)
                    link(4, dve.tensor_tensor(T3[:, :], PMN[:, :, 0], PMN[:, :, 1], ALU.max))
                if part == 2:
                    after(4)
                    link(5, dve.tensor_tensor(T2[:, :], T2[:, :], T3[:, :], ALU.max))
                    after(5)
                    link(6, dve.tensor_tensor(GE[:, :, 0:GROUPS], T1[:, :].rearrange("p (t g) -> p t g", g=GROUPS),
                                              T2[:, :].rearrange("p (t g) -> p t g", g=GROUPS), ALU.add))
                    after(6)
                    dve.memset(junk[:, :], 0.0)
                    for t in range(CT):
                        i = dve.max(out=GM[:, t, :], in_=GE[:, t, :])
                    link(7, i)
                if part == 3:
                    after(7)
                    dve.memset(junk[:, :], 0.0)
                    for t in range(CT):
                        i = dve.match_replace(out=GR[:, t, :], in_to_replace=GM[:, t, :], in_values=GE[:, t, :], imm_value=-BIG)
                    link(8, i)
                    after(8)
                    link(9, dve.tensor_scalar(GMK[:, :, :], GR[:, :, 0:GROUPS], -BIG / 3, None, ALU.is_lt))
                    after(9)
                    gm = GMK[:, :, :].rearrange("p t g -> p (t g)").unsqueeze(2).broadcast_to([P, CT * GROUPS, EPG])
                    link(10, dve.tensor_tensor(T4[:, :, :].rearrange("p t (g e) -> p (t g) e", e=EPG),
                                               SBI[:, :, :].rearrange("p t (g e) -> p (t g) e", e=EPG), gm, ALU.mult))
                if part == 4:
                    after(10)
                    gm = GMK[:, :, :].unsqueeze(3).broadcast_to([P, CT, GROUPS, EPG])
                    link(11, dve.scalar_tensor_tensor(
                        out=T4[:, :, :].rearrange("p t (g e) -> p t g e", e=EPG), in0=gm, scalar=-1.0,
                        in1=T4[:, :, :].rearrange("p t (g e) -> p t g e", e=EPG), op0=ALU.add, op1=ALU.add))
                    after(11)
                    link(12, dve.tensor_copy(ME[:, :, 0:EXPERTS], T4[:, :, :]))
                    after(12)
                    dve.memset(junk[:, :], 0.0)
                    for t in range(CT):
                        i = dve.max(out=EM[:, t, :], in_=ME[:, t, :])
                    link(13, i)
                if part == 5:
                    after(13)
                    dve.memset(junk[:, :], 0.0)
                    for t in range(CT):
                        i = dve.match_replace(out=ER[:, t, :], in_to_replace=EM[:, t, :], in_values=ME[:, t, :], imm_value=-BIG)
                    link(14, i)
                    after(14)
                    link(15, dve.scalar_tensor_tensor(out=W[:, :, :], in0=ER[:, :, 0:EXPERTS], scalar=-BIG / 3,
                                                      in1=SC[:, :, :], op0=ALU.is_lt, op1=ALU.mult))
                if part == 6:
                    after(15)
                    link(16, dve.tensor_reduce(SM[:, :], W[:, :, :], AX.X, ALU.add))
                    after(16)
                    link(17, dve.tensor_scalar(SME[:, :], SM[:, :], 1e-20, None, ALU.add))
                    after(17)
                    link(18, dve.reciprocal(RSM[:, :], SME[:, :]))
                if part == 7:
                    after(18)
                    link(19, dve.scalar_tensor_tensor(out=C[:, :, :], in0=W[:, :, :], scalar=0.5 * ROUTE_SCALE,
                                                      in1=RSM[:, :].unsqueeze(2).broadcast_to([P, CT, EXPERTS]),
                                                      op0=ALU.mult, op1=ALU.mult))
                    after(19)
                    dve.tensor_copy(CTK[:, :, 0:EXPERTS].bitcast(f32r), C[:, :, :]).then_inc(A.cth, 1)
                    dve.wait_ge(A.cth, c + 1)
                    dve.tensor_tensor(CTK[:, :, EXPERTS:2 * EXPERTS].bitcast(f32r), C[:, :, :], CTK[:, :, 0:EXPERTS],
                                      ALU.subtract).then_inc(A.ct, 1)

            def attention(k, A, L, Lnext):
                def body(c, cur, prev):
                    for g in range(SLOTS):
                        n = c * SLOTS + g
                        if cur and g == 4:
                            dve.wait_ge(A.vm, c + 1)
                            if prev:
                                dve.wait_ge(A.pv, n - 4)
                            elif k == 0:
                                dve.wait_ge(s_pc, 4)
                            dst = V[:, :, :, 0:HD]
                            src = TP[:, :].rearrange("p (t h c) -> p t h c", t=CT, h=H)
                            if k == 0:
                                dve.tensor_copy(dst, src).then_inc(A.vd, 1)
                            else:
                                for t in range(CT):
                                    i = dve.tensor_tensor(dst[:, t], src[:, t], BV[:, :, :], ALU.add)
                                i.then_inc(A.vd, 1)
                        if prev and g == 6:
                            norm_apply(Lnext, c - 1)
                        if prev and g == 7:
                            low_half(Lnext, c - 1)
                        if k == 1 and (cur if g >= 3 else prev):
                            hg, b = group_of(g, 3)
                            dve.wait_ge(A.mt, n - 2)
                            if g >= 5 or prev:
                                dve.wait_ge(A.s2, 4 * (n - 4))
                            dve.tensor_tensor(Q2[:, (g + 1) % 2, :], MT[:, 0:SEQ], QS[:, hg, SEQ * b:SEQ * (b + 1)].bitcast(f32),
                                              ALU.add).then_inc(A.q2, 1)
                        if cur:
                            hg, b = group_of(g, 0)
                            if k == 0:
                                dve.wait_ge(A.rl, n + 1)
                                if g >= 2 or prev:
                                    dve.wait_ge(A.qs, n - 1)
                                dve.scalar_tensor_tensor(out=PHI[:, 2 + g % 2, :], in0=PHI[:, 0, :], scalar=1.0,
                                                         in1=PHI[:, 1, :], op0=ALU.min, op1=ALU.add).then_inc(A.ph, 1)
                            else:
                                dve.wait_ge(A.hp, n + 1)
                                if prev:
                                    dve.wait_ge(A.s2, 4 * (n - b - 6))
                                dve.scalar_tensor_tensor(out=(KS if b else QS)[:, hg, :], in0=PJ[:, :],
                                                         scalar=COL[:, 4 * b + hg:4 * b + hg + 1],
                                                         in1=HP[:, g % 2, :].bitcast(f32), op0=ALU.add, op1=ALU.subtract)\
                                   .then_inc(A.qs, 1)
                        if prev and g == 5:
                            dve.wait_ge(A.e2, c)
                            dve.wait_ge(A.bo, c)
                            dve.tensor_tensor(tiles(c - 1).rearrange("p a d -> p (a d)"), TP[:, :],
                                              tiles(c - 1).rearrange("p a d -> p (a d)"), ALU.add).then_inc(A.res, 1)
                            dve.wait_ge(A.res, c)
                            norm_stats(Lnext, c - 1)
                            norm_aggregate(Lnext, c - 1)
                        for h in range(4):
                            if cur if g >= 2 else prev:
                                dve.wait_ge(A.s1, 4 * (n - 2) + h + 1)
                                if k == 0:
                                    if h == 0 and (g >= 4 or prev):
                                        dve.wait_ge(A.pv, n - 3)
                                    if h == 0 and g == 2 and not prev:
                                        dve.wait_ge(s_qkl, 1)
                                        dve.wait_ge(s_sel, 1)
                                    dve.tensor_tensor(PT[:, g % 2, h, 0:3 * P], S[h][:, 0:3 * P],
                                                      MASK[:, :, :].rearrange("p a b -> p (a b)"), ALU.mult).then_inc(A.mk, 1)
                                else:
                                    if h == 0 and (g >= 3 or prev):
                                        dve.wait_ge(A.mt, n - 2)
                                    dve.tensor_reduce(MEXP[:, :, 32 * h + 3 * HD], S[h][:, :].rearrange("p (t k) -> p t k", t=2),
                                                      AX.X, ALU.max).then_inc(A.mx, 1)
                            if prev and g == 7:
                                route(A, c - 1, 2 * h)
                                route(A, c - 1, 2 * h + 1)
                        if g % 2 == 0 and (cur if g >= 6 else prev):
                            hg, _ = group_of(g, 6)
                            j = c * HG + (g - 6) // 2
                            o = TP[:, :].rearrange("p (t h c) -> p t h c", t=CT, h=4)
                            dve.wait_ge(A.nt, j + 1)
                            if k == 0:
                                dve.tensor_scalar(DEN[:, :, :], o[:, :, :, HD], DEN_EPS, None, ALU.add).then_inc(A.dn, 1)
                                dve.wait_ge(A.dn, j + 1)
                                dve.reciprocal(RDEN[:, :, :], DEN[:, :, :]).then_inc(A.rd, 1)
                            else:
                                dve.reciprocal(RDEN[:, :, :], o[:, :, :, HD]).then_inc(A.rd, 1)
                            dve.wait_ge(A.rd, j + 1)
                            if hg == 0 and prev:
                                dve.wait_ge(A.e1, c)
                            dve.tensor_tensor(OTOK[:, :, 32 * hg:32 * (hg + 1)].rearrange("p t (h c) -> p t h c", h=4),
                                              o[:, :, :, 0:HD], RDEN[:, :, :].unsqueeze(3).broadcast_to([P, CT, 4, HD]),
                                              ALU.mult).then_inc(A.nm, 1)

                chunks(dve, body)

            def experts(k, F, Lnext):
                def body(c, cur, prev):
                    for u in range(UNITS):
                        n = c * UNITS + u
                        if cur:
                            t, ab, gg = TH[:, u % 2, :], AB[:, u % 2, :], GG[:, u % 3, :]
                            dve.wait_ge(F.th, n + 1)
                            dve.scalar_tensor_tensor(out=ab, in0=t, scalar=1.0, in1=G[u % 2][:, :], op0=ALU.add,
                                                     op1=ALU.mult).then_inc(F.a, 1)
                            dve.wait_ge(F.a, n + 1)
                            dve.wait_ge(F.u, n + 1)
                            dve.tensor_tensor(ab, ab, U[u % 2][:, :], ALU.mult).then_inc(F.b, 1)
                            dve.wait_ge(F.b, n + 1)
                            if u >= 3 or prev:
                                dve.wait_ge(F.gl, n - 2)
                            if u < EXPERTS:
                                dve.wait_ge(F.c, c * EXPERTS + u + 1)
                                dve.tensor_tensor(gg, ab, CBC[u % 2][:, :], ALU.mult).then_inc(F.gg, 1)
                            else:
                                dve.tensor_scalar(gg, ab, 0.5, None, ALU.mult).then_inc(F.gg, 1)
                        if prev and u == 5:
                            dve.wait_ge(F.e1, c)
                            dve.tensor_tensor(tiles(c - 1).rearrange("p a d -> p (a d)"), TP[:, :],
                                              tiles(c - 1).rearrange("p a d -> p (a d)"), ALU.add).then_inc(F.res, 1)
                            if k == 0:
                                dve.wait_ge(F.res, c)
                                norm_stats(Lnext, c - 1)
                        if k == 0 and prev and u == 6:
                            norm_aggregate(Lnext, c - 1)
                        if k == 0 and prev and u == 8:
                            norm_apply(Lnext, c - 1)
                        if k == 0 and prev and u == 11:
                            low_half(Lnext, c - 1)

                chunks(dve, body)

            attention(0, AT[0], LN[0], LN[1])
            experts(0, FF[0], LN[2])
            attention(1, AT[1], LN[2], LN[3])
            experts(1, FF[1], None)


_INS = ['L0_attn_a_x', 'L0_attn_a_Wq', 'L0_attn_a_Wk', 'L0_attn_a_Wv', 'L0_attn_a_Wo', 'L0_attn_a_bo', 'L0_attn_b_Wqkv',
        'L0_attn_b_bqkv', 'L0_attn_b_Wo', 'L0_attn_b_bo', 'L0_ffn_router_w', 'L0_ffn_bias', 'L0_ffn_gate_w', 'L0_ffn_up_w',
        'L0_ffn_down_w', 'L0_ffn_sh_gate_w', 'L0_ffn_sh_up_w', 'L0_ffn_sh_down_w']
_OUTS = [((8, 256, 128), 'float32')]


def kernel(**inputs):
    import numpy as _np
    import concourse.bacc as _bacc
    from concourse import mybir as _mybir
    from concourse.bass_utils import run_bass_kernel_spmd as _run

    nc = _bacc.Bacc("TRN2", target_bir_lowering=False, num_devices=1)
    arrays, args = {}, []
    for name in _INS:
        a = _np.ascontiguousarray(inputs[name])
        arrays[f"in_{name}_dram"] = a
        args.append(nc.dram_tensor(f"in_{name}_dram", a.shape, _mybir.dt.from_np(a.dtype), kind="ExternalInput").ap())
    shape, dtype = _OUTS[0]
    out = nc.dram_tensor("out_0_dram", shape, _mybir.dt.from_np(_np.dtype(dtype)), kind="ExternalOutput").ap()
    hybrid_block(nc, args, out)
    r = _run(nc, [arrays], core_ids=[0])
    return r.results[0]["out_0_dram"]
```

```python
import concourse.bass as bass
from concourse import mybir
from contextlib import ExitStack


class NormSems:

    def __init__(self, sem, prefix):
        self.st = sem(prefix + "st")
        self.mv = sem(prefix + "mv")
        self.ve = sem(prefix + "ve")
        self.rs = sem(prefix + "rs")
        self.xn = sem(prefix + "xn")
        self.xt = sem(prefix + "xt")
        self.xs = sem(prefix + "xs")
        self.xl = sem(prefix + "xl")


class AttentionSems:

    def __init__(self, sem, prefix):
        self.xv = sem(prefix + "xv")
        self.vm = sem(prefix + "vm")
        self.vd = sem(prefix + "vd")
        self.bo = sem(prefix + "bo")
        self.pj = sem(prefix + "pj")
        self.rl = sem(prefix + "rl")
        self.ph = sem(prefix + "ph")
        self.hp = sem(prefix + "hp")
        self.qs = sem(prefix + "qs")
        self.s1 = sem(prefix + "s1")
        self.mk = sem(prefix + "mk")
        self.mt = sem(prefix + "mt")
        self.q2 = sem(prefix + "q2")
        self.mx = sem(prefix + "mx")
        self.s2 = sem(prefix + "s2")
        self.ex = sem(prefix + "ex")
        self.pv = sem(prefix + "pv")
        self.ot = sem(prefix + "ot")
        self.nt = sem(prefix + "nt")
        self.dn = sem(prefix + "dn")
        self.rd = sem(prefix + "rd")
        self.nm = sem(prefix + "nm")
        self.e1 = sem(prefix + "e1")
        self.ott = sem(prefix + "ott")
        self.e2 = sem(prefix + "e2")
        self.res = sem(prefix + "res")
        self.e4 = sem(prefix + "e4")
        self.th = sem(prefix + "th")
        self.e5 = sem(prefix + "e5")
        self.rv = sem(prefix + "rv")
        self.cth = sem(prefix + "cth")
        self.ct = sem(prefix + "ct")
        self.cb = sem(prefix + "cb")


class ExpertSems:

    def __init__(self, sem, prefix):
        self.g = sem(prefix + "g")
        self.u = sem(prefix + "u")
        self.c = sem(prefix + "c")
        self.th = sem(prefix + "th")
        self.a = sem(prefix + "a")
        self.b = sem(prefix + "b")
        self.gg = sem(prefix + "gg")
        self.gh = sem(prefix + "gh")
        self.gl = sem(prefix + "gl")
        self.d = sem(prefix + "d")
        self.yt = sem(prefix + "yt")
        self.e1 = sem(prefix + "e1")
        self.res = sem(prefix + "res")


def hybrid_block(nc, ins, out):
    f32 = mybir.dt.float32
    f32r = mybir.dt.float32r
    ALU = mybir.AluOpType
    ACT = mybir.ActivationFunctionType
    AX = mybir.AxisListType

    (x_in, wq_a, wk_a, wv_a, wo_a, bo_a, wqkv_b, bqkv_b, wo_b, bo_b,
     router_w, router_bias, gate_w, up_w, down_w, sh_gate, sh_up, sh_down) = ins

    P = 128
    BATCH, SEQ, DM = x_in.shape
    TOKENS = BATCH * SEQ
    TILES = TOKENS // P
    CT = 4
    CHUNK = CT * P
    CHUNKS = TILES // CT
    H = 16
    HD = DM // H
    HG = 4
    BPC = CHUNK // SEQ
    SLOTS = HG * BPC
    EXPERTS = router_w.shape[0]
    UNITS = EXPERTS + 2
    GROUPS, TOP_GROUPS, TOP_K = 4, 2, 4
    EPG = EXPERTS // GROUPS
    ROUTE_SCALE = 2.5
    LN_EPS = 1e-5
    DEN_EPS = 1e-5
    SOFTMAX_SCALE = float(HD) ** -0.5
    BIG = 3e38
    PIECES, UPP = 6, 3

    x_tiles = x_in.rearrange("b (t p) d -> p (b t) d", p=P)
    out_tiles = out.rearrange("b (t p) d -> p (b t) d", p=P)

    ctx = ExitStack()
    with ctx:
        def sb(name, shape, dt=f32):
            return ctx.enter_context(nc.sbuf_tensor(name, shape, dt))

        def sem(name):
            return ctx.enter_context(nc.semaphore(name))

        X = sb("X", [P, TILES, DM])
        XH = sb("XH", [P, TOKENS], f32r)
        XL = sb("XL", [P, TOKENS], f32r)
        CB = sb("CB", [2 * EXPERTS, TOKENS], f32r)
        WH = sb("WH", [P, UNITS, 3, P], f32r)
        WL = sb("WL", [P, UNITS, 3, P], f32r)
        stage = sb("stage", [P, 2, UPP, 3, P])
        SEL = sb("SEL", [2 * EXPERTS, EXPERTS, P], f32r)
        QS = sb("QS", [P, HG, CHUNK], f32r)
        KS = sb("KS", [P, HG, CHUNK], f32r)
        Q2 = sb("Q2", [P, 2, SEQ], f32r)
        PT = sb("PT", [P, 2, 4, CHUNK])
        V = sb("V", [P, CT, H, 32])
        PHI = sb("PHI", [P, 4, CHUNK])
        HP = sb("HP", [P, 2, CHUNK], f32r)
        OTS = sb("OTS", [P, CHUNK])
        OTOK = sb("OTOK", [P, CT, DM])
        OTT = sb("OTT", [P, CHUNK])
        XN = sb("XN", [P, CT, DM])
        XS = sb("XS", [P, CHUNK])
        XV = sb("XV", [P, CHUNK])
        MEXP = sb("MEXP", [P, 2, P])
        MASK = sb("MASK", [P, 3, P])
        nat = stage[:, 0, :, :, :].rearrange("p a b c -> p (a b) c")
        QKR = PT[:, 0, :, :].rearrange("p a (h c) -> p a h c", c=32)
        SELR = PT[0:2 * EXPERTS, 1, :, :].rearrange("p a (e c) -> p (a e) c", c=P)
        QKH = sb("QKH", [P, 4, H * 32], f32r)
        QKL = sb("QKL", [P, 4, H * 32], f32r)
        WV = sb("WV", [P, 2, DM])
        WO = sb("WO", [P, 2, DM])
        RT = sb("RT", [P, EXPERTS])
        BO = sb("BO", [P, 2, DM])
        BV = sb("BV", [P, H, HD])
        RB = sb("RB", [P, EXPERTS])
        BROW = sb("BROW", [1, 3 * DM])
        SROW = sb("SROW", [1, 2, H * 32])
        MROW = sb("MROW", [1, 2, P])
        COL = sb("COL", [P, 10])
        BCM = sb("BCM", [P, 8])
        ident = sb("ident", [P, P])
        STT_ = sb("LNST", [P, CT, 6])
        MV = sb("MV", [P, CT, 2])
        VE = sb("VE", [P, CT])
        RS = sb("RS", [P, CT])
        ST0 = sb("ST0", [P, TILES, 6])
        MV0 = sb("MV0", [P, TILES, 2])
        VE0 = sb("VE0", [P, TILES])
        RS0 = sb("RS0", [P, TILES])
        NH = sb("NH", [P, CT])
        EPS = sb("EPS", [P, CT])
        junk = sb("junk", [P, 1])
        route_junk = sb("route_junk", [P, 1])
        DEN = sb("DEN", [P, CT, 4])
        RDEN = sb("RDEN", [P, CT, 4])
        TH64 = sb("TH64", [P, TILES, EXPERTS])
        SC = sb("SC", [P, CT, EXPERTS])
        SBI = sb("SBI", [P, CT, EXPERTS])
        PMX = sb("PMX", [P, CT * GROUPS, 2])
        PMN = sb("PMN", [P, CT * GROUPS, 2])
        T1 = sb("T1", [P, CT * GROUPS])
        T2 = sb("T2", [P, CT * GROUPS])
        T3 = sb("T3", [P, CT * GROUPS])
        GE = sb("GE", [P, CT, GROUPS + 8 - TOP_GROUPS])
        GM = sb("GM", [P, CT, 8])
        GR = sb("GR", [P, CT, GROUPS + 8 - TOP_GROUPS])
        GMK = sb("GMK", [P, CT, GROUPS])
        T4 = sb("T4", [P, CT, EXPERTS])
        ME = sb("ME", [P, CT, EXPERTS + 8 - TOP_K])
        EM = sb("EM", [P, CT, 8])
        ER = sb("ER", [P, CT, EXPERTS + 8 - TOP_K])
        W = sb("W", [P, CT, EXPERTS])
        SM = sb("SM", [P, CT])
        SME = sb("SME", [P, CT])
        RSM = sb("RSM", [P, CT])
        C = sb("C", [P, CT, EXPERTS])
        CTK = sb("CTK", [P, CT, 2 * EXPERTS])
        TH = PT[:, 0, 0:2, :]
        AB = PT[:, 0, 2:4, :]
        GG = PT[:, 1, 0:3, :]
        GH = QS[:, 1:4, :]
        GL = KS[:, 1:4, :]

        BANK = [ctx.enter_context(nc.psum_tensor(f"bank{i}", [P, 512], f32)) for i in range(8)]
        S = BANK[0:4]
        OT, PJ, MT, TP = BANK[4:8]
        G = BANK[0:2]
        U = BANK[2:4]
        CBC = BANK[4:6]
        XN0 = [XN, OTOK, XN, OTOK]
        TP0 = [BANK[7], BANK[6], BANK[4], BANK[3]]
        Y = BANK[6]

        s_x0 = sem("x_first_chunk_loaded")
        s_x = sem("x_rest_loaded")
        s_nat = sem("small_weights_loaded")
        s_row = sem("bias_row_loaded")
        s_bc = sem("broadcasts_loaded")
        s_raw = [sem(f"piece{p}_loaded") for p in range(PIECES)]
        s_wh = sem("piece_high_done")
        s_wl = sem("piece_low_done")
        s_id = sem("ident_done")
        s_pc = sem("pool_constants_done")
        s_wt = sem("weights_transposed")
        s_w0 = sem("bank0_unpacked")
        s_w1 = sem("bank1_unpacked")
        s_row2s = sem("rows_cleared")
        s_row2 = sem("rows_done")
        s_sel = sem("selectors_done")
        s_col = sem("columns_transposed")
        s_cd = sem("columns_done")
        s_qkh = sem("qk_high_done")
        s_qkl = sem("qk_low_done")
        s_out = sem("stored")

        LN = [NormSems(sem, f"ln{k}_") for k in range(4)]
        AT = [AttentionSems(sem, f"at{k}_") for k in range(2)]
        FF = [ExpertSems(sem, f"ff{k}_") for k in range(2)]

        def ch(t, c, n):
            return t[:, bass.ds(c * n, n)]

        def tiles(c):
            return X[:, bass.ds(c * CT, CT), :]

        def flat(ap):
            return ap.rearrange("p a b c -> p (a b c)")

        def group_of(g, lag):
            return ((g - lag) % SLOTS) // BPC, (g - lag) % BPC

        ROUTE_UNIT = 3
        ROUTE_PARTS = 8
        SCORE_LAG = [3, 2]
        LATE_SLOTS = {0: (4,), 2: (5,), 5: (6,), 8: (7,)}
        LATE_UNITS = {0: (0,), 1: (1,), 2: (2, 3), 3: (4, 5, 6), 4: (7, 8), 5: (9, 10), 6: (11,)}

        def layers(eng, slot, unit):
            for k in range(2):
                for g in range(SLOTS):
                    if k == 1:
                        for u in LATE_UNITS.get(g, ()):
                            unit(0, CHUNKS, u, False, True, False)
                    slot(k, 0, g, True, False)
                with eng.Fori(1, CHUNKS) as c:
                    for g in range(SLOTS):
                        slot(k, c, g, True, True)
                for g in range(4):
                    slot(k, CHUNKS, g, False, True)
                for u in range(UNITS):
                    for g in LATE_SLOTS.get(u, ()):
                        slot(k, CHUNKS, g, False, True)
                    unit(k, 0, u, True, False, True)
                with eng.Fori(1, CHUNKS - 1) as c:
                    for u in range(UNITS):
                        unit(k, c, u, True, True, True)
                for u in range(UNITS):
                    unit(k, CHUNKS - 1, u, True, True, False)
            for u in range(12):
                unit(1, CHUNKS, u, False, True, False)

        block = ctx.enter_context(nc.Block())

        @block.sync
        def _(sp):
            sp.dma_start(X[:, 0:CT, :], x_tiles[:, 0:CT, :]).then_inc(s_x0, 16)
            for m, w in enumerate((wq_a, wk_a, wv_a, wo_a)):
                sp.dma_start(nat[:, m, :], w).then_inc(s_nat, 16)
            sp.dma_start(X[:, CT:TILES, :], x_tiles[:, CT:TILES, :]).then_inc(s_x, 16)

            def piece(p):
                dst = stage[:, p % 2, :, :, :]
                if p == 0:
                    sp.wait_ge(s_wt, 1)
                if p >= 2:
                    sp.wait_ge(s_wl, p - 1)
                e0 = p * UPP
                n = min(UPP, EXPERTS - e0)
                for k, w in enumerate((gate_w, up_w, down_w)):
                    sp.dma_start(dst[:, 0:n, k, :], w[e0:e0 + n].rearrange("e d f -> d e f")).then_inc(s_raw[p], 16)
                if n < UPP:
                    for k, w in enumerate((sh_gate, sh_up)):
                        sp.dma_start(dst[:, n:UPP, k, :], w.rearrange("d (a f) -> d a f", a=2)).then_inc(s_raw[p], 16)
                    sp.dma_start(dst[:, n:UPP, 2, :], sh_down.rearrange("(a f) d -> f a d", a=2)).then_inc(s_raw[p], 16)

            for p in range(PIECES):
                piece(p)
            with sp.Fori(0, CHUNKS) as c:
                sp.wait_ge(FF[1].res, c + 1)
                sp.dma_start(out_tiles[:, bass.ds(c * CT, CT), :], X[:, bass.ds(c * CT, CT), :]).then_inc(s_out, 16)
            sp.wait_ge(s_out, 16 * CHUNKS)

        @block.gpsimd
        def _(pool):
            pool.memset(ident[:, :], 0.0).then_inc(s_id, 1)
            pool.wait_ge(s_id, 1)
            pool.affine_select(out=ident[:, :], in_=ident[:, :], compare_op=ALU.not_equal, fill=1.0, base=0,
                               pattern=[[-1, P]], channel_multiplier=1).then_inc(s_id, 1)
            pool.memset(NH[:, :], -0.5)
            pool.memset(EPS[:, :], LN_EPS)
            pool.memset(QKR, 0.0).then_inc(s_pc, 1)
            pool.wait_ge(s_pc, 1)
            for c in range(CHUNKS):
                pool.wait_ge(LN[0].mv, c + 1)
                pool.tensor_tensor(VE0[:, c * CT:(c + 1) * CT], MV0[:, c * CT:(c + 1) * CT, 1], EPS[:, :], ALU.add)\
                    .then_inc(LN[0].ve, 1)
                pool.wait_ge(LN[0].ve, c + 1)
                pool.tensor_tensor(RS0[:, c * CT:(c + 1) * CT], VE0[:, c * CT:(c + 1) * CT], NH[:, :], ALU.pow)\
                    .then_inc(LN[0].rs, 1)
            pool.memset(V[:, :, :, :], 0.0)
            pool.memset(MEXP[:, :, :], 0.0)
            pool.memset(GE[:, :, :], BIG)
            pool.memset(ME[:, :, :], BIG)
            pool.memset(SELR, 0.0)
            pool.memset(MASK[:, :, :], 1.0).then_inc(s_pc, 1)
            pool.wait_ge(s_pc, 2)
            pool.memset(V[:, :, :, HD:HD + 1], 1.0)
            for k in (0, 2):
                pool.affine_select(out=MASK[:, k, :], in_=MASK[:, k, :], compare_op=ALU.is_ge, fill=0.0, base=0,
                                   pattern=[[1, P]], channel_multiplier=-1)
            for k in range(2):
                pool.affine_select(out=SELR, in_=SELR, compare_op=ALU.not_equal, fill=1.0, base=-EXPERTS * k,
                                   pattern=[[-1, EXPERTS], [0, P]], channel_multiplier=1).then_inc(s_pc, 1)
                pool.wait_ge(s_pc, 3 + k)

            def norm_pool(L, c):
                pool.wait_ge(L.mv, c + 1)
                pool.tensor_tensor(VE[:, :], MV[:, :, 1], EPS[:, :], ALU.add).then_inc(L.ve, 1)
                pool.wait_ge(L.ve, c + 1)
                pool.tensor_tensor(RS[:, :], VE[:, :], NH[:, :], ALU.pow).then_inc(L.rs, 1)

            def slot(k, c, g, cur, prev):
                A, L, Lnext = AT[k], LN[2 * k], LN[2 * k + 1]
                n = c * SLOTS + g
                if k == 0 and not prev and g >= SLOTS - PIECES:
                    p = g - (SLOTS - PIECES)
                    part = slice(UPP * p, UPP * (p + 1))
                    pool.wait_ge(s_wh, p + 1)
                    pool.tensor_tensor(flat(WL[:, part, :, :]), flat(stage[:, p % 2, :, :, :]),
                                       flat(WH[:, part, :, :]).bitcast(f32), ALU.subtract).then_inc(s_wl, 1)
                if cur:
                    hg, b = group_of(g, 0)
                    pool.wait_ge(A.hp, n + 1)
                    if prev:
                        pool.wait_ge(A.s1 if k == 0 else A.s2, 4 * (n - b - 6))
                    elif k == 1 and g == 2:
                        pool.wait_ge(FF[0].d, UNITS * CHUNKS)
                    pool.tensor_tensor((KS if b else QS)[:, hg, :], PHI[:, 2 + g % 2, :],
                                       HP[:, g % 2, :].bitcast(f32), ALU.subtract).then_inc(A.qs, 1)
                if cur and g == 1:
                    pool.wait_ge(L.xl, c + 1)
                    if prev:
                        pool.wait_ge(A.vm, c)
                    pool.tensor_tensor(XV[:, :], ch(XH, c, CHUNK).bitcast(f32), ch(XL, c, CHUNK).bitcast(f32),
                                       ALU.add).then_inc(A.xv, 1)
                if cur and g == 2:
                    if k == 0 and not prev:
                        pool.wait_ge(s_bc, 16 * 4)
                    pool.tensor_tensor(tiles(c), tiles(c), BO[:, k, :].unsqueeze(1).broadcast_to([P, CT, DM]),
                                       ALU.add).then_inc(A.bo, 1)
                if prev and g == 5:
                    norm_pool(Lnext, c - 1)
                if prev and g == 7:
                    pool.wait_ge(Lnext.xs, c)
                    pool.tensor_tensor(ch(XL, c - 1, CHUNK), XS[:, :], ch(XH, c - 1, CHUNK).bitcast(f32),
                                       ALU.subtract).then_inc(Lnext.xl, 1)

            def unit(k, c, u, cur, prev, more):
                F = FF[k]
                n = c * UNITS + u
                if cur if u >= 1 else prev:
                    pool.wait_ge(F.gh, n)
                    if u >= 4 or prev:
                        pool.wait_ge(F.d, n - 3)
                    pool.tensor_tensor(GL[:, (u - 1) % 3, :], GG[:, (u - 1) % 3, :],
                                       GH[:, (u - 1) % 3, :].bitcast(f32), ALU.subtract).then_inc(F.gl, 1)
                if prev and u == 7 and k == 0:
                    norm_pool(LN[2], c - 1)

            layers(pool, slot, unit)

        @block.scalar
        def _(act):
            for m in range(3):
                act.dma_start(nat[:, 4 + m, :], wqkv_b[m * P:(m + 1) * P, :]).then_inc(s_nat, 16)
            act.dma_start(nat[:, 7, :], wo_b).then_inc(s_nat, 16)
            act.dma_start(nat[0:EXPERTS, 8, :], router_w).then_inc(s_nat, 16)
            act.dma_start(BROW[:, :], bqkv_b.rearrange("(a n) -> a n", a=1)).then_inc(s_row, 16)
            act.dma_start(BO[:, 0, :], bo_a.partition_broadcast(P)).then_inc(s_bc, 16)
            act.dma_start(BO[:, 1, :], bo_b.partition_broadcast(P)).then_inc(s_bc, 16)
            act.dma_start(RB[:, :], router_bias.partition_broadcast(P)).then_inc(s_bc, 16)
            act.dma_start(BV[:, :, :], bqkv_b.rearrange("(h c) -> h c", h=H)[:, 2 * HD:3 * HD].partition_broadcast(P))\
               .then_inc(s_bc, 16)
            act.wait_ge(s_w0, 1)
            act.activation(QKH[:, 0:2, :], QKR[:, 0:2].rearrange("p a h c -> p a (h c)"), ACT.Copy).then_inc(s_qkh, 1)

            def first_high_half(c):
                act.wait_ge(LN[0].xt, c + 1)
                act.activation(XH[:, c * CHUNK:(c + 1) * CHUNK], TP0[c][:, :], ACT.Copy).then_inc(LN[0].xs, 1)

            first_high_half(0)
            act.wait_ge(s_wt, 1)
            act.wait_ge(s_pc, 1)
            wqkv_t = BANK[1][:, 0:3 * DM].rearrange("p (h c) -> p h c", h=H)
            for s in range(3):
                act.activation(QKR[:, 2, :, HD * s:HD * (s + 1)], wqkv_t[:, :, 0:HD], ACT.Copy)
                act.activation(QKR[:, 3, :, HD * s:HD * (s + 1)], wqkv_t[:, :, HD:2 * HD], ACT.Copy)
            act.activation(WV[:, 1, :].rearrange("p (h c) -> p h c", h=H), wqkv_t[:, :, 2 * HD:3 * HD], ACT.Copy)
            act.activation(WO[:, 1, :], BANK[1][:, 3 * DM:4 * DM], ACT.Copy).then_inc(s_w1, 1)
            act.wait_ge(s_w1, 1)
            act.activation(QKH[:, 2:4, :], QKR[:, 2:4].rearrange("p a h c -> p a (h c)"), ACT.Copy).then_inc(s_qkh, 1)
            for c in range(1, CHUNKS):
                first_high_half(c)

            def halves(L, c, router):
                act.wait_ge(L.xt, c + 1)
                i = act.activation(ch(XH, c, CHUNK), TP[:, :], ACT.Copy)
                if router:
                    i = act.activation(XS[:, :], TP[:, :], ACT.Copy)
                i.then_inc(L.xs, 1)

            def slot(k, c, g, cur, prev):
                A, L, Lnext = AT[k], LN[2 * k], LN[2 * k + 1]
                n = c * SLOTS + g
                hg, b = group_of(g, 0)
                if k == 0 and not prev and g >= SLOTS - PIECES:
                    p = g - (SLOTS - PIECES)
                    act.wait_ge(s_raw[p], 16 * (6 if p == PIECES - 1 else 3))
                    act.activation(flat(WH[:, UPP * p:UPP * (p + 1), :, :]), flat(stage[:, p % 2, :, :, :]),
                                   ACT.Copy).then_inc(s_wh, 1)
                if prev and g == 5:
                    act.wait_ge(A.e1, c)
                    act.activation(OTT[:, :], TP[:, :], ACT.Copy).then_inc(A.ott, 1)
                def router_tanh():
                    act.wait_ge(A.e4, c)
                    act.activation(TH64[:, bass.ds((c - 1) * CT, CT), :].rearrange("p a b -> p (a b)"),
                                   TP[:, 0:CT * EXPERTS], ACT.Tanh, scale=0.5).then_inc(A.th, 1)

                def probabilities(h):
                    if not (cur if g >= 3 else prev):
                        return
                    if h == 0 and g == 3 and not prev:
                        act.wait_ge(FF[0].gl, UNITS * CHUNKS)
                    act.wait_ge(A.s2, 4 * (n - 3) + h + 1)
                    if h == 0 and (g >= 5 or prev):
                        act.wait_ge(A.pv, n - 4)
                    act.activation(PT[:, (g + 1) % 2, h, :], S[h][:, :], ACT.Exp, scale=SOFTMAX_SCALE).then_inc(A.ex, 1)

                def output():
                    if g % 2 == 1 and (cur if g >= 4 else prev):
                        act.wait_ge(A.pv, n - 3)
                        if g >= 7 or prev:
                            act.wait_ge(A.nt, c * HG + (g - 5) // 2)
                        act.activation(OTS[:, :], OT[:, :], ACT.Copy).then_inc(A.ot, 1)

                if k == 0:
                    if cur:
                        act.wait_ge(A.pj, n + 1)
                        if g or prev:
                            act.wait_ge(A.ph, n)
                        act.activation(PHI[:, 0, :], PJ[:, :], ACT.Exp)
                        act.activation(PHI[:, 1, :], PJ[:, :], ACT.Relu).then_inc(A.rl, 1)
                    if prev and g == 7:
                        halves(Lnext, c - 1, True)
                    if cur:
                        if g == 0 and not prev:
                            act.wait_ge(s_cd, 1)
                        act.wait_ge(A.ph, n + 1)
                        if g >= 2 or prev:
                            act.wait_ge(A.qs, n - 1)
                        act.activation(HP[:, g % 2, :], PHI[:, 2 + g % 2, :], ACT.Identity,
                                       scale=COL[:, 8 + b:9 + b]).then_inc(A.hp, 1)
                    output()
                    if prev and g == 7:
                        router_tanh()
                else:
                    if cur:
                        act.wait_ge(A.pj, n + 1)
                        if g >= 2 or prev:
                            act.wait_ge(A.qs, n - 1)
                        if g == 0 and not prev:
                            act.wait_ge(s_cd, 2)
                        act.activation(PHI[:, 2 + g % 2, :], PJ[:, :], ACT.Identity, bias=COL[:, 4 * b + hg:4 * b + hg + 1])
                        act.activation(HP[:, g % 2, :], PJ[:, :], ACT.Identity, bias=BCM[:, 4 * b + hg:4 * b + hg + 1],
                                       scale=COL[:, 8 + b:9 + b]).then_inc(A.hp, 1)
                    if prev and g == 7:
                        halves(Lnext, c - 1, True)
                    for h in range(4):
                        probabilities(h)
                    output()
                    if prev and g == 7:
                        router_tanh()
                if prev and not cur and g == 3:
                    act.wait_ge(A.e5, 1)
                    act.activation(ch(CB, 0, CHUNK), TP[0:2 * EXPERTS, :], ACT.Copy).then_inc(A.cb, 1)

            def unit(k, c, u, cur, prev, more):
                F, A = FF[k], AT[k]
                n = c * UNITS + u
                if cur:
                    act.wait_ge(F.g, n + 1)
                    if u >= 2 or prev:
                        act.wait_ge(F.a, n - 1)
                    if u == 0 and not prev:
                        act.wait_ge(A.pv, SLOTS * CHUNKS)
                    act.activation(TH[:, u % 2, :], G[u % 2][:, :], ACT.Tanh, scale=0.5).then_inc(F.th, 1)
                if cur if u >= 1 else prev:
                    act.wait_ge(F.gg, n)
                    if u >= 4 or prev:
                        act.wait_ge(F.d, n - 3)
                    act.activation(GH[:, (u - 1) % 3, :], GG[:, (u - 1) % 3, :], ACT.Copy).then_inc(F.gh, 1)
                if prev and u == 2:
                    act.wait_ge(F.d, UNITS * c)
                    act.activation(OTT[:, :], Y[:, :], ACT.Copy).then_inc(F.yt, 1)
                if prev and u == 10 and k == 0:
                    halves(LN[2], c - 1, False)
                if more and u == 15:
                    act.wait_ge(A.e5, c + 2)
                    act.activation(ch(CB, c + 1, CHUNK), TP[0:2 * EXPERTS, :], ACT.Copy).then_inc(A.cb, 1)

            layers(act, slot, unit)

        @block.tensor
        def _(pe):
            def three(out, wh, wl, vh, vl, start=True, stop=True):
                pe.matmul(out, wh, vh, start=start, stop=False)
                pe.matmul(out, wh, vl, start=False, stop=False)
                return pe.matmul(out, wl, vh, start=False, stop=stop)

            pe.wait_ge(s_id, 2)
            pe.wait_ge(s_nat, 16 * 9)
            for m in range(8):
                pe.transpose(BANK[m // 4][:, P * (m % 4):P * (m % 4 + 1)], nat[:, m, :], ident[:, :])
            pe.transpose(BANK[3][:, 0:EXPERTS], nat[0:EXPERTS, 8, :], ident[0:EXPERTS, 0:EXPERTS]).then_inc(s_wt, 1)

            def turn(L, c):
                for t in range(CT):
                    i = pe.transpose(TP[:, P * t:P * (t + 1)], XN[:, t, :], ident[:, :])
                i.then_inc(L.xt, 1)

            def first_turn(c):
                pe.wait_ge(LN[0].xn, c + 1)
                for t in range(CT):
                    i = pe.transpose(TP0[c][:, P * t:P * (t + 1)], XN0[c][:, t, :], ident[:, :])
                i.then_inc(LN[0].xt, 1)

            first_turn(0)
            pe.wait_ge(s_row2, 1)
            for w in range(2):
                for hg in range(HG):
                    pe.matmul(BANK[2][:, 16 + 4 * w + hg:17 + 4 * w + hg], SROW[:, w, P * hg:P * (hg + 1)], ident[0:1, 0:1],
                              start=True, stop=True)
                i = pe.matmul(BANK[2][:, 24 + w:25 + w], MROW[:, w, :], ident[0:1, 0:1], start=True, stop=True)
            i.then_inc(s_col, 1)
            for c in range(1, CHUNKS):
                if c == 3:
                    pe.wait_ge(s_w0, 1)
                first_turn(c)
            pe.wait_ge(s_qkl, 1)

            def slot(k, c, g, cur, prev):
                A, L, Lnext = AT[k], LN[2 * k], LN[2 * k + 1]
                done, rows = (A.mk, 3 * HD) if k == 0 else (A.ex, 3 * HD + 1)
                n = c * SLOTS + g

                def projection():
                    if not cur:
                        return
                    hg, b = group_of(g, 0)
                    if g == 0:
                        pe.wait_ge(L.xl, c + 1)
                        if k == 1 and not prev:
                            pe.wait_ge(s_qkl, 2)
                            pe.wait_ge(FF[0].gg, UNITS * CHUNKS - 2)
                    if g or prev:
                        pe.wait_ge(A.rl if k == 0 else A.hp, n)
                    w = slice(P * hg, P * (hg + 1))
                    three(PJ[:, :], QKH[:, 2 * k + b, w], QKL[:, 2 * k + b, w], ch(XH, c, CHUNK), ch(XL, c, CHUNK))\
                        .then_inc(A.pj, 1)

                def scores():
                    lag = SCORE_LAG[k]
                    if not (cur if g >= lag else prev):
                        return
                    hg, b = group_of(g, lag)
                    pe.wait_ge(A.qs, c * SLOTS + (g - lag) // 2 * 2 + 2)
                    if k == 1 and g == 2 and not prev:
                        pe.wait_ge(FF[0].b, UNITS * CHUNKS)
                    if k == 0 and g == 3 and not prev:
                        pe.wait_ge(s_w1, 1)
                        pe.wait_ge(s_cd, 1)
                        pe.wait_ge(L.xl, CHUNKS)
                    for h in range(4):
                        r = slice(32 * h, 32 * h + 3 * HD)
                        if k == 0:
                            if g >= 4 or prev:
                                pe.wait_ge(A.mk, 4 * (n - 4) + h + 1)
                            pe.matmul(S[h][:, 0:SEQ], KS[r, hg, SEQ * b:SEQ * b + P], QS[r, hg, SEQ * b:SEQ * (b + 1)],
                                      start=True, stop=True)
                            i = pe.matmul(S[h][:, SEQ:SEQ + P], KS[r, hg, SEQ * b + P:SEQ * (b + 1)],
                                          QS[r, hg, SEQ * b + P:SEQ * (b + 1)], start=True, stop=True)
                        else:
                            if g >= 4 or prev:
                                pe.wait_ge(A.ex, 4 * (n - 4) + h + 1)
                            elif g == 3:
                                pe.wait_ge(A.mx, 4 * (n - 3) + h + 1)
                            for t in range(2):
                                i = pe.matmul(S[h][:, SEQ * t:SEQ * (t + 1)],
                                              QS[r, hg, SEQ * b + P * t:SEQ * b + P * (t + 1)],
                                              KS[r, hg, SEQ * b:SEQ * (b + 1)], start=True, stop=True)
                        i.then_inc(A.s1, 1)

                def maxima():
                    if not (cur if g >= 3 else prev):
                        return
                    pe.wait_ge(A.mx, 4 * (n - 2))
                    if g >= 4 or prev:
                        pe.wait_ge(A.q2, n - 3)
                    else:
                        pe.wait_ge(FF[0].yt, CHUNKS)
                    for t in range(2):
                        i = pe.transpose(MT[:, P * t:P * (t + 1)], MEXP[:, t, :], ident[:, :])
                    i.then_inc(A.mt, 1)

                def scores_less_maxima(heads):
                    if not (cur if g >= 3 else prev):
                        return
                    hg, b = group_of(g, 3)
                    pe.wait_ge(A.q2, n - 2)
                    for h in heads:
                        r = slice(32 * h, 32 * h + rows)
                        if cur or g < 2:
                            pe.wait_ge(A.mx, 4 * (n - 2) + h + 1)
                        else:
                            pe.wait_ge(A.ex, 4 * (n - 4) + h + 1)
                        for t in range(2):
                            i = pe.matmul(S[h][:, SEQ * t:SEQ * (t + 1)],
                                          KS[r, hg, SEQ * b + P * t:SEQ * b + P * (t + 1)],
                                          Q2[r, (g + 1) % 2, :], start=True, stop=True)
                        i.then_inc(A.s2, 1)

                def values_product(kt):
                    if not (cur if g >= 4 else prev):
                        return
                    hg, b = group_of(g, 4)
                    if kt == 0:
                        pe.wait_ge(done, 4 * (n - 3))
                        if g == 4 and cur:
                            pe.wait_ge(A.vd, c + 1)
                        if b == 0 and (g > 4 or prev):
                            pe.wait_ge(A.ot, c * HG + (g - 4) // 2)
                    q0 = kt * P if k == 0 else 0
                    for h in range(4):
                        src = PT[:, g % 2, h, SEQ * kt:SEQ * (kt + 1) - q0]
                        i = pe.matmul(OT[32 * h:32 * (h + 1), SEQ * b + q0:SEQ * (b + 1)],
                                      V[:, 2 * b + kt, 4 * hg + h, :], src, start=(kt == 0), stop=(kt == 1),
                                      skip_group_check=True)
                    if kt == 1:
                        i.then_inc(A.pv, 1)

                def middle():
                    if g % 2 == 0 and (cur if g >= 6 else prev):
                        j = c * HG + (g - 6) // 2
                        pe.wait_ge(A.ot, j + 1)
                        if g == 0:
                            if cur:
                                pe.wait_ge(A.rl if k == 0 else A.hp, n + 1)
                            else:
                                pe.wait_ge(A.th, c - 1)
                        if g <= 2:
                            pe.wait_ge(A.nm, j)
                        if g == 4 and cur:
                            pe.wait_ge(A.vd, c + 1)
                        if g == 4 and not cur:
                            pe.wait_ge(A.cb, 1)
                        if g == 6 and not prev:
                            pe.wait_ge(A.vd, 1)
                            if k == 1:
                                pe.wait_ge(L.xl, CHUNKS)
                        if g == 6 and prev:
                            pe.wait_ge(A.res, c)
                        for t in range(CT):
                            i = pe.transpose(TP[:, P * t:P * (t + 1)], OTS[:, P * t:P * (t + 1)], ident[:, :])
                        i.then_inc(A.nt, 1)
                    if g == 3:
                        if prev:
                            pe.wait_ge(A.nm, c * HG - 1)
                        elif k == 1:
                            pe.wait_ge(FF[0].res, CHUNKS)
                    if cur and g == 3:
                        pe.wait_ge(A.xv, c + 1)
                        for t in range(CT):
                            i = pe.matmul(TP[:, P * t:P * (t + 1)], XV[:, P * t:P * (t + 1)], WV[:, k, :],
                                          start=True, stop=True)
                        i.then_inc(A.vm, 1)
                    if not cur and g == 3:
                        routing_weights(A, 0)
                    if prev and g == 5:
                        pe.wait_ge(A.ott, c)
                        for t in range(CT):
                            i = pe.matmul(TP[:, P * t:P * (t + 1)], OTT[:, P * t:P * (t + 1)], WO[:, k, :],
                                          start=True, stop=True)
                        i.then_inc(A.e2, 1)
                    if prev and g == 7:
                        pe.wait_ge(Lnext.xn, c)
                        if cur:
                            pe.wait_ge(A.nm, c * HG + 1)
                        turn(Lnext, c - 1)

                if k == 0:
                    if g in (3,5):
                        scores()
                        projection()
                    else:
                        projection()
                        scores()
                    middle()
                    values_product(0)
                    values_product(1)
                elif g in (1,3,5,7):
                    maxima()
                    scores()
                    projection()
                    middle()
                    values_product(0)
                    values_product(1)
                    scores_less_maxima(range(4))
                else:
                    maxima()
                    projection()
                    scores()
                    middle()
                    values_product(0)
                    scores_less_maxima((0, 1))
                    values_product(1)
                    scores_less_maxima((2, 3))
                if prev and g == 4:
                    pe.wait_ge(A.nm, c * HG)
                    for t in range(CT):
                        i = pe.transpose(TP[:, P * t:P * (t + 1)], OTOK[:, t, :], ident[:, :])
                    i.then_inc(A.e1, 1)
                if prev and g == 7:
                    pe.wait_ge(Lnext.xs, c)
                    for t in range(CT):
                        i = pe.matmul(TP[:, EXPERTS * t:EXPERTS * (t + 1)], XS[:, P * t:P * (t + 1)], RT[:, :],
                                      start=True, stop=True)
                    i.then_inc(A.e4, 1)

            def routing_weights(A, c):
                pe.wait_ge(A.ct, c + 1)
                for t in range(CT):
                    i = pe.transpose(TP[0:2 * EXPERTS, P * t:P * (t + 1)], CTK[:, t, :], ident[:, :])
                i.then_inc(A.e5, 1)

            def unit(k, c, u, cur, prev, more):
                F, A, L = FF[k], AT[k], LN[2 * k + 1]
                n = c * UNITS + u
                if cur:
                    if u == 0:
                        pe.wait_ge(L.xl, c + 1)
                        pe.wait_ge(A.cb, c + 1)
                    if u == 0 and not prev:
                        pe.wait_ge(A.mk if k == 0 else A.ex, 4 * SLOTS * CHUNKS)
                        pe.wait_ge(A.ot, HG * CHUNKS)
                        pe.wait_ge(A.hp, SLOTS * CHUNKS)
                        if k == 0:
                            pe.wait_ge(s_wl, PIECES)
                        else:
                            pe.wait_ge(A.q2, SLOTS * CHUNKS)
                    vh, vl = ch(XH, c, CHUNK), ch(XL, c, CHUNK)
                    if u >= 2 or prev:
                        pe.wait_ge(F.a, n - 1)
                    three(G[u % 2][:, :], WH[:, u, 0, :], WL[:, u, 0, :], vh, vl).then_inc(F.g, 1)
                    if u >= 2 or prev:
                        pe.wait_ge(F.b, n - 1)
                    if u < EXPERTS:
                        if u >= 2:
                            pe.wait_ge(F.gg, n - 1)
                        elif prev:
                            pe.wait_ge(F.gg, n - 3)
                    three(U[u % 2][:, :], WH[:, u, 1, :], WL[:, u, 1, :], vh, vl).then_inc(F.u, 1)
                    if u < EXPERTS:
                        pe.matmul(CBC[u % 2][:, :], SEL[:, u, :], ch(CB, c, CHUNK), start=True, stop=True).then_inc(F.c, 1)
                if cur if u >= 3 else prev:
                    du = (u - 3) % UNITS
                    pe.wait_ge(F.gl, n - 2)
                    if du == 0 and prev:
                        pe.wait_ge(F.yt, c)
                    three(Y[:, :], WH[:, du, 2, :], WL[:, du, 2, :], GH[:, du % 3, :], GL[:, du % 3, :],
                          start=(du == 0), stop=(du == UNITS - 1)).then_inc(F.d, 1)
                if prev and u == 4:
                    pe.wait_ge(F.yt, c)
                    for t in range(CT):
                        i = pe.transpose(TP[:, P * t:P * (t + 1)], OTT[:, P * t:P * (t + 1)], ident[:, :])
                    i.then_inc(F.e1, 1)
                if prev and u == 9 and k == 0:
                    pe.wait_ge(LN[2].xn, c)
                    if not cur:
                        pe.wait_ge(AT[1].vd, 1)
                    turn(LN[2], c - 1)
                if more and u == 14:
                    if prev:
                        pe.wait_ge(LN[2].xl if k == 0 else F.res, c)
                    else:
                        pe.wait_ge(A.th, CHUNKS)
                    routing_weights(A, c + 1)

            layers(pe, slot, unit)

        @block.vector
        def _(dve):
            dve.memset(SROW[:, :, :], 0.0)
            dve.memset(MROW[:, :, :], 0.0).then_inc(s_row2s, 1)
            dve.wait_ge(s_row2s, 1)
            srow = SROW[:, :, :].rearrange("p w (h c) -> p w h c", h=H)
            mrow = MROW[:, :, :].rearrange("p w (h c) -> p w h c", h=4)
            brow = BROW[:, :].rearrange("p (h c) -> p h c", h=H)
            dve.memset(srow[:, 1, :, 3 * HD:3 * HD + 1], -1.0)
            dve.memset(mrow[:, 0, :, 2 * HD:3 * HD], 1.0)
            dve.memset(mrow[:, 1, :, HD:2 * HD], 1.0)
            def norm_stats(L, c):
                dve.memset(junk[:, :], 0.0)
                for t in range(CT):
                    i = dve.bn_stats(out=STT_[:, t, :], in_=X[:, bass.ds(c * CT + t, 1), :].rearrange("p a d -> p (a d)"))
                i.then_inc(L.st, 1)

            def norm_aggregate(L, c):
                dve.wait_ge(L.st, c + 1)
                dve.memset(junk[:, :], 0.0)
                for t in range(CT):
                    i = dve.bn_aggr(out=MV[:, t, :], in_=STT_[:, t, :])
                i.then_inc(L.mv, 1)

            def norm_apply(L, c):
                dve.wait_ge(L.mv, c + 1)
                dve.wait_ge(L.rs, c + 1)
                for t in range(CT):
                    i = dve.tensor_scalar(XN[:, t, :], X[:, bass.ds(c * CT + t, 1), :].rearrange("p a d -> p (a d)"),
                                          MV[:, t, 0:1], RS[:, t:t + 1], ALU.subtract, ALU.mult)
                i.then_inc(L.xn, 1)

            def low_half(L, c):
                dve.wait_ge(L.xs, c + 1)
                dve.tensor_tensor(ch(XL, c, CHUNK), TP[:, :], ch(XH, c, CHUNK).bitcast(f32), ALU.subtract).then_inc(L.xl, 1)

            for c in range(CHUNKS):
                dve.wait_ge(s_x if c else s_x0, 16)
                for t in range(c * CT, (c + 1) * CT):
                    i = dve.bn_stats(out=ST0[:, t, :], in_=X[:, t, :])
                i.then_inc(LN[0].st, 1)
                dve.wait_ge(LN[0].st, c + 1)
                for t in range(c * CT, (c + 1) * CT):
                    i = dve.bn_aggr(out=MV0[:, t, :], in_=ST0[:, t, :])
                i.then_inc(LN[0].mv, 1)

            def first_apply(c):
                dve.wait_ge(LN[0].mv, c + 1)
                dve.wait_ge(LN[0].rs, c + 1)
                if c >= 2:
                    dve.wait_ge(LN[0].xt, c - 1)
                for t in range(CT):
                    j = c * CT + t
                    i = dve.tensor_scalar(XN0[c][:, t, :], X[:, j, :], MV0[:, j, 0:1], RS0[:, j:j + 1],
                                          ALU.subtract, ALU.mult)
                i.then_inc(LN[0].xn, 1)

            def first_low_half(c):
                dve.wait_ge(LN[0].xs, c + 1)
                part = slice(c * CHUNK, (c + 1) * CHUNK)
                dve.tensor_tensor(XL[:, part], TP0[c][:, :], XH[:, part].bitcast(f32), ALU.subtract).then_inc(LN[0].xl, 1)

            def qk_low(k):
                dve.wait_ge(s_qkh, k + 1)
                dve.tensor_tensor(QKL[:, 2 * k:2 * k + 2, :], QKR[:, 2 * k:2 * k + 2].rearrange("p a h c -> p a (h c)"),
                                  QKH[:, 2 * k:2 * k + 2, :].bitcast(f32), ALU.subtract).then_inc(s_qkl, 1)

            dve.wait_ge(s_row, 16)
            for w in range(2):
                for s in range(3):
                    i = dve.tensor_copy(srow[:, w, :, HD * s:HD * (s + 1)], brow[:, :, HD * w:HD * (w + 1)])
            i.then_inc(s_row2, 1)
            first_apply(0)
            dve.wait_ge(s_wt, 1)
            dve.wait_ge(s_pc, 1)
            for w in range(2):
                src = BANK[0][:, DM * w:DM * (w + 1)].rearrange("p (h c) -> p h c", h=H)
                for s in range(3):
                    dve.tensor_copy(QKR[:, w, :, HD * s:HD * (s + 1)], src)
            dve.tensor_copy(WV[:, 0, :], BANK[0][:, 2 * DM:3 * DM])
            dve.tensor_copy(WO[:, 0, :], BANK[0][:, 3 * DM:4 * DM])
            dve.tensor_copy(RT[:, :], BANK[3][:, 0:EXPERTS]).then_inc(s_w0, 1)
            qk_low(0)
            first_low_half(0)
            first_apply(1)
            dve.wait_ge(s_col, 1)
            dve.tensor_copy(COL[:, :], BANK[2][:, 16:26]).then_inc(s_cd, 1)
            first_apply(2)
            first_low_half(1)
            first_apply(3)
            first_low_half(2)
            first_low_half(3)
            dve.wait_ge(s_cd, 1)
            for w in range(2):
                i = dve.tensor_scalar(BCM[:, 4 * w:4 * (w + 1)], COL[:, 4 * w:4 * (w + 1)], COL[:, 8 + w:9 + w], None, ALU.mult)
            i.then_inc(s_cd, 1)
            qk_low(1)
            dve.wait_ge(s_pc, 4)
            dve.tensor_copy(SEL[:, :, :], SELR).then_inc(s_sel, 1)


            LINKS = 19

            def route(A, c, part):
                base = c * LINKS

                def link(k, instr):
                    instr.then_inc(A.rv, 1)

                def after(k):
                    dve.wait_ge(A.rv, base + k)

                sbi4 = SBI[:, :, :].rearrange("p t (g i j) -> p (t g) i j", i=2, j=2)
                if part == 0:
                    dve.wait_ge(A.th, c + 1)
                    link(1, dve.tensor_scalar(SC[:, :, :], TH64[:, bass.ds(c * CT, CT), :], 0.5, 0.5, ALU.mult, ALU.add))
                    after(1)
                    link(2, dve.tensor_tensor(SBI[:, :, :], SC[:, :, :], RB[:, :].unsqueeze(1).broadcast_to([P, CT, EXPERTS]),
                                              ALU.add))
                if part == 1:
                    after(2)
                    dve.tensor_tensor(PMX[:, :, :], sbi4[:, :, :, 0], sbi4[:, :, :, 1], ALU.max)
                    link(3, dve.tensor_tensor(PMN[:, :, :], sbi4[:, :, :, 0], sbi4[:, :, :, 1], ALU.min))
                    after(3)
                    dve.tensor_tensor(T1[:, :], PMX[:, :, 0], PMX[:, :, 1], ALU.max)
                    dve.tensor_tensor(T2[:, :], PMX[:, :, 0], PMX[:, :, 1], ALU.min)
                    link(4, dve.tensor_tensor(T3[:, :], PMN[:, :, 0], PMN[:, :, 1], ALU.max))
                if part == 2:
                    after(4)
                    link(5, dve.tensor_tensor(T2[:, :], T2[:, :], T3[:, :], ALU.max))
                    after(5)
                    link(6, dve.tensor_tensor(GE[:, :, 0:GROUPS], T1[:, :].rearrange("p (t g) -> p t g", g=GROUPS),
                                              T2[:, :].rearrange("p (t g) -> p t g", g=GROUPS), ALU.add))
                    after(6)
                    dve.memset(route_junk[:, :], 0.0)
                    for t in range(CT):
                        i = dve.max(out=GM[:, t, :], in_=GE[:, t, :])
                    link(7, i)
                if part == 3:
                    after(7)
                    dve.memset(route_junk[:, :], 0.0)
                    for t in range(CT):
                        i = dve.match_replace(out=GR[:, t, :], in_to_replace=GM[:, t, :], in_values=GE[:, t, :], imm_value=-BIG)
                    link(8, i)
                    after(8)
                    link(9, dve.tensor_scalar(GMK[:, :, :], GR[:, :, 0:GROUPS], -BIG / 3, None, ALU.is_lt))
                    after(9)
                    gm = GMK[:, :, :].rearrange("p t g -> p (t g)").unsqueeze(2).broadcast_to([P, CT * GROUPS, EPG])
                    link(10, dve.tensor_tensor(T4[:, :, :].rearrange("p t (g e) -> p (t g) e", e=EPG),
                                               SBI[:, :, :].rearrange("p t (g e) -> p (t g) e", e=EPG), gm, ALU.mult))
                if part == 4:
                    after(10)
                    gm = GMK[:, :, :].unsqueeze(3).broadcast_to([P, CT, GROUPS, EPG])
                    link(11, dve.scalar_tensor_tensor(
                        out=T4[:, :, :].rearrange("p t (g e) -> p t g e", e=EPG), in0=gm, scalar=-1.0,
                        in1=T4[:, :, :].rearrange("p t (g e) -> p t g e", e=EPG), op0=ALU.add, op1=ALU.add))
                    after(11)
                    link(12, dve.tensor_copy(ME[:, :, 0:EXPERTS], T4[:, :, :]))
                    after(12)
                    dve.memset(route_junk[:, :], 0.0)
                    for t in range(CT):
                        i = dve.max(out=EM[:, t, :], in_=ME[:, t, :])
                    link(13, i)
                if part == 5:
                    after(13)
                    dve.memset(route_junk[:, :], 0.0)
                    for t in range(CT):
                        i = dve.match_replace(out=ER[:, t, :], in_to_replace=EM[:, t, :], in_values=ME[:, t, :], imm_value=-BIG)
                    link(14, i)
                    after(14)
                    link(15, dve.scalar_tensor_tensor(out=W[:, :, :], in0=ER[:, :, 0:EXPERTS], scalar=-BIG / 3,
                                                      in1=SC[:, :, :], op0=ALU.is_lt, op1=ALU.mult))
                if part == 6:
                    after(15)
                    link(16, dve.tensor_reduce(SM[:, :], W[:, :, :], AX.X, ALU.add))
                    after(16)
                    link(17, dve.tensor_scalar(SME[:, :], SM[:, :], 1e-20, None, ALU.add))
                    after(17)
                    link(18, dve.reciprocal(RSM[:, :], SME[:, :]))
                if part == 7:
                    after(18)
                    link(19, dve.scalar_tensor_tensor(out=C[:, :, :], in0=W[:, :, :], scalar=0.5 * ROUTE_SCALE,
                                                      in1=RSM[:, :].unsqueeze(2).broadcast_to([P, CT, EXPERTS]),
                                                      op0=ALU.mult, op1=ALU.mult))
                    after(19)
                    dve.tensor_copy(CTK[:, :, 0:EXPERTS].bitcast(f32r), C[:, :, :]).then_inc(A.cth, 1)
                    dve.wait_ge(A.cth, c + 1)
                    dve.tensor_tensor(CTK[:, :, EXPERTS:2 * EXPERTS].bitcast(f32r), C[:, :, :], CTK[:, :, 0:EXPERTS],
                                      ALU.subtract).then_inc(A.ct, 1)

            def slot(k, c, g, cur, prev):
                A, L, Lnext = AT[k], LN[2 * k], LN[2 * k + 1]
                n = c * SLOTS + g
                hg, b = group_of(g, 0)
                if k == 1 and (cur if g >= 3 else prev):
                    qhg, qb = group_of(g, 3)
                    dve.wait_ge(A.mt, n - 2)
                    if g >= 5 or prev:
                        dve.wait_ge(A.s2, 4 * (n - 4))
                    dve.tensor_tensor(Q2[:, (g + 1) % 2, :], MT[:, 0:SEQ], QS[:, qhg, SEQ * qb:SEQ * (qb + 1)].bitcast(f32),
                                      ALU.add).then_inc(A.q2, 1)
                if cur and g == 4:
                    dve.wait_ge(A.vm, c + 1)
                    if prev:
                        dve.wait_ge(A.pv, n - 4)
                    elif k == 0:
                        dve.wait_ge(s_pc, 4)
                    dst = V[:, :, :, 0:HD]
                    src = TP[:, :].rearrange("p (t h c) -> p t h c", t=CT, h=H)
                    if k == 0:
                        dve.tensor_copy(dst, src).then_inc(A.vd, 1)
                    else:
                        dve.tensor_tensor(dst, src, BV[:, :, :].unsqueeze(1).broadcast_to([P, CT, H, HD]),
                                          ALU.add).then_inc(A.vd, 1)
                def head(h):
                    lag = SCORE_LAG[k]
                    if not (cur if g >= lag else prev):
                        return
                    dve.wait_ge(A.s1, 4 * (n - lag) + h + 1)
                    if k == 0:
                        if h == 0 and (g >= 5 or prev):
                            dve.wait_ge(A.pv, n - 4)
                        if h == 0 and g == 3 and not prev:
                            dve.wait_ge(s_qkl, 2)
                            dve.wait_ge(s_sel, 1)
                        dve.tensor_tensor(PT[:, (g + 1) % 2, h, 0:3 * P], S[h][:, 0:3 * P],
                                          MASK[:, :, :].rearrange("p a b -> p (a b)"), ALU.mult).then_inc(A.mk, 1)
                    else:
                        if h == 0 and (g >= 3 or prev):
                            dve.wait_ge(A.mt, n - 2)
                        dve.tensor_reduce(MEXP[:, :, 32 * h + 3 * HD], S[h][:, :].rearrange("p (t k) -> p t k", t=2),
                                          AX.X, ALU.max).then_inc(A.mx, 1)

                def middle():
                    if prev and g == 6:
                        norm_apply(Lnext, c - 1)
                    if prev and g == 5:
                        dve.wait_ge(A.e2, c)
                        dve.wait_ge(A.bo, c)
                        dve.tensor_tensor(tiles(c - 1).rearrange("p a d -> p (a d)"), TP[:, :],
                                          tiles(c - 1).rearrange("p a d -> p (a d)"), ALU.add).then_inc(A.res, 1)
                        dve.wait_ge(A.res, c)
                        norm_stats(Lnext, c - 1)
                    if g % 2 == 0 and (cur if g >= 6 else prev):
                        ohg, _ = group_of(g, 6)
                        j = c * HG + (g - 6) // 2
                        o = TP[:, :].rearrange("p (t h c) -> p t h c", t=CT, h=4)
                        dve.wait_ge(A.nt, j + 1)
                        if k == 0:
                            dve.tensor_scalar(DEN[:, :, :], o[:, :, :, HD], DEN_EPS, None, ALU.add).then_inc(A.dn, 1)
                            dve.wait_ge(A.dn, j + 1)
                            dve.reciprocal(RDEN[:, :, :], DEN[:, :, :]).then_inc(A.rd, 1)
                        else:
                            dve.reciprocal(RDEN[:, :, :], o[:, :, :, HD]).then_inc(A.rd, 1)
                        dve.wait_ge(A.rd, j + 1)
                        if ohg == 0 and prev:
                            dve.wait_ge(A.e1, c)
                        dve.tensor_tensor(OTOK[:, :, 32 * ohg:32 * (ohg + 1)].rearrange("p t (h c) -> p t h c", h=4),
                                          o[:, :, :, 0:HD], RDEN[:, :, :].unsqueeze(3).broadcast_to([P, CT, 4, HD]),
                                          ALU.mult).then_inc(A.nm, 1)

                head(0)
                head(1)
                if k == 1:
                    middle()
                head(2)
                if k == 1 and prev and g == 5:
                    norm_aggregate(Lnext, c - 1)
                head(3)
                if cur and k == 0:
                    dve.wait_ge(A.rl, n + 1)
                    if g >= 2 or prev:
                        dve.wait_ge(A.qs, n - 1)
                    dve.scalar_tensor_tensor(out=PHI[:, 2 + g % 2, :], in0=PHI[:, 0, :], scalar=1.0,
                                             in1=PHI[:, 1, :], op0=ALU.min, op1=ALU.add).then_inc(A.ph, 1)
                if k == 0:
                    middle()
                    if prev and g == 5:
                        norm_aggregate(Lnext, c - 1)
                if not cur and g < 4:
                    for part in range(2 * g, 2 * g + 2):
                        route(A, 0, part)

            def unit(k, c, u, cur, prev, more):
                F = FF[k]
                n = c * UNITS + u
                if cur:
                    t, ab, gg = TH[:, u % 2, :], AB[:, u % 2, :], GG[:, u % 3, :]
                    dve.wait_ge(F.th, n + 1)
                    dve.scalar_tensor_tensor(out=ab, in0=t, scalar=1.0, in1=G[u % 2][:, :], op0=ALU.add,
                                             op1=ALU.mult).then_inc(F.a, 1)
                    dve.wait_ge(F.a, n + 1)
                    dve.wait_ge(F.u, n + 1)
                    dve.tensor_tensor(ab, ab, U[u % 2][:, :], ALU.mult).then_inc(F.b, 1)
                    dve.wait_ge(F.b, n + 1)
                    if u >= 3 or prev:
                        dve.wait_ge(F.gl, n - 2)
                    if u < EXPERTS:
                        dve.wait_ge(F.c, c * EXPERTS + u + 1)
                        dve.tensor_tensor(gg, ab, CBC[u % 2][:, :], ALU.mult).then_inc(F.gg, 1)
                    else:
                        dve.tensor_scalar(gg, ab, 0.5, None, ALU.mult).then_inc(F.gg, 1)
                if prev and u == 5:
                    dve.wait_ge(F.e1, c)
                    dve.tensor_tensor(tiles(c - 1).rearrange("p a d -> p (a d)"), TP[:, :],
                                      tiles(c - 1).rearrange("p a d -> p (a d)"), ALU.add).then_inc(F.res, 1)
                    if k == 0:
                        dve.wait_ge(F.res, c)
                        norm_stats(LN[2], c - 1)
                if k == 0 and prev and u == 6:
                    norm_aggregate(LN[2], c - 1)
                if k == 0 and prev and u == 8:
                    norm_apply(LN[2], c - 1)
                if k == 0 and prev and u == 11:
                    low_half(LN[2], c - 1)
                if more and ROUTE_UNIT <= u < ROUTE_UNIT + ROUTE_PARTS:
                    route(AT[k], c + 1, u - ROUTE_UNIT)

            layers(dve, slot, unit)


_INS = ['L0_attn_a_x', 'L0_attn_a_Wq', 'L0_attn_a_Wk', 'L0_attn_a_Wv', 'L0_attn_a_Wo', 'L0_attn_a_bo', 'L0_attn_b_Wqkv',
        'L0_attn_b_bqkv', 'L0_attn_b_Wo', 'L0_attn_b_bo', 'L0_ffn_router_w', 'L0_ffn_bias', 'L0_ffn_gate_w', 'L0_ffn_up_w',
        'L0_ffn_down_w', 'L0_ffn_sh_gate_w', 'L0_ffn_sh_up_w', 'L0_ffn_sh_down_w']
_OUTS = [((8, 256, 128), 'float32')]


def kernel(**inputs):
    import numpy as _np
    import concourse.bacc as _bacc
    from concourse import mybir as _mybir
    from concourse.bass_utils import run_bass_kernel_spmd as _run

    nc = _bacc.Bacc("TRN2", target_bir_lowering=False, num_devices=1)
    arrays, args = {}, []
    for name in _INS:
        a = _np.ascontiguousarray(inputs[name])
        arrays[f"in_{name}_dram"] = a
        args.append(nc.dram_tensor(f"in_{name}_dram", a.shape, _mybir.dt.from_np(a.dtype), kind="ExternalInput").ap())
    shape, dtype = _OUTS[0]
    out = nc.dram_tensor("out_0_dram", shape, _mybir.dt.from_np(_np.dtype(dtype)), kind="ExternalOutput").ap()
    hybrid_block(nc, args, out)
    r = _run(nc, [arrays], core_ids=[0])
    return r.results[0]["out_0_dram"]
```
